# Optimizing a Trainium2 kernel written in Bass

```python
import numpy as np
import jax
import jax.numpy as jnp

def _softmax(x, axis=-1):
    return jax.nn.softmax(x, axis=axis)

def _gelu(x):
    return jax.nn.gelu(x, approximate=True)

def _silu(x):
    return jax.nn.silu(x)

def _sigmoid(x):
    return jax.nn.sigmoid(x)

def _layernorm(x, axis=-1, eps=1e-05):
    m = jnp.mean(x, axis=axis, keepdims=True)
    v = jnp.var(x, axis=axis, keepdims=True)
    return (x - m) / jnp.sqrt(v + eps)

def _scatter_add(tgt, idx, src, axis=0):
    return tgt.at[idx].add(src)

def _segment_sum(src, seg, n):
    return jax.ops.segment_sum(src, seg, n)
kernel_name = 'mk_xattn_ffn_d1_seqx_r4_e65c50'

def setup_inputs(seed: int=0):
    np.random.seed(seed)
    _w = jnp.asarray

    def _rec_inputs():
        import jax
        import jax.numpy as jnp
        _rk = jax.random.key(seed)
        x = -0.000125 + 0.9999 * jax.random.normal(jax.random.fold_in(_rk, 1), (4, 512, 512), jnp.float32)
        _lenS = 512 - jax.random.randint(jax.random.fold_in(_rk, 7), (4,), 0, max(1, 512 // 4) + 1, jnp.int32)
        _lenS2 = 512 - jax.random.randint(jax.random.fold_in(_rk, 8), (4,), 0, max(1, 512 // 4) + 1, jnp.int32)
        fside_BxS2xS2_0 = -3.05549e-07 + 0.0199987 * jax.random.normal(jax.random.fold_in(_rk, 11), (4, 512, 512), jnp.float32)
        _ctx_1024P = jax.random.normal(jax.random.fold_in(_rk, 12), (4, 16, 256), jnp.float32)
        _ctx_1024c = jax.random.dirichlet(jax.random.fold_in(_rk, 512), 0.3 * jnp.ones((16,), jnp.float32), (4, 512))
        _ctx_1024t = jnp.einsum('bsk,bkd->bsd', _ctx_1024c, _ctx_1024P)
        _ctx_1024t = _ctx_1024t * jax.lax.rsqrt(jnp.mean(jnp.square(_ctx_1024t)) + 1e-12) * 0.953939
        ctx_1024 = 6.82029e-06 + 0.0200006 * (_ctx_1024t + 0.3 * jax.random.normal(jax.random.fold_in(_rk, 612), (4, 512, 256), jnp.float32))
        return (x, fside_BxS2xS2_0, ctx_1024)
    x, fside_BxS2xS2_0, ctx_1024 = _rec_inputs()

    def _L0_xattn_setup():
        import jax, jax.numpy as jnp
        import numpy as np
        EPS = 1e-06
        QMAX = 127.0

        def _smooth_quant_linear(x, w):
            amax_x = jnp.max(jnp.abs(x), axis=0)
            amax_w = jnp.max(jnp.abs(w), axis=0)
            s = jnp.sqrt(jnp.maximum(amax_x, EPS) / jnp.maximum(amax_w, EPS))
            s = jnp.maximum(s, EPS)
            xs = x / s
            ws = w * s
            x_scale = jnp.maximum(jnp.max(jnp.abs(xs), axis=-1, keepdims=True), EPS) / QMAX
            w_scale = jnp.maximum(jnp.max(jnp.abs(ws), axis=-1, keepdims=True), EPS) / QMAX
            x_q = jnp.clip(jnp.round(xs / x_scale), -QMAX, QMAX)
            w_q = jnp.clip(jnp.round(ws / w_scale), -QMAX, QMAX)
            return x_q @ w_q.T * x_scale * w_scale.T

        def _expert_forward(xe, guw, dw):
            h = _smooth_quant_linear(xe, guw)
            gate, up = jnp.split(h, 2, axis=-1)
            a = jax.nn.silu(gate) * up
            return _smooth_quant_linear(a, dw)
        key = jax.random.key(seed)
        k1, k2, k3 = jax.random.split(key, 3)
        E, T, D, I = (8, 512, 512, 256)
        x = jax.random.normal(k1, (E, T, D), dtype=jnp.float32)
        gate_up_weight = jax.random.normal(k2, (E, 2 * I, D), dtype=jnp.float32) * 0.02
        down_weight = jax.random.normal(k3, (E, D, I), dtype=jnp.float32) * 0.02
        return {'x': x, 'gate_up_weight': gate_up_weight, 'down_weight': down_weight}
    _L0_xattn_all = _L0_xattn_setup()
    _L0_xattn_in = {k: v for k, v in _L0_xattn_all.items() if k in ()}
    del _L0_xattn_all

    def _L0_ffn_setup():
        import jax, jax.numpy as jnp
        import numpy as np
        NUM_EXPERTS = 8
        EXPERTS_PER_TOK = 2
        key = jax.random.key(seed)
        k1, k2, k3, k4, k5 = jax.random.split(key, 5)
        B, T, D, F, E = (4, 256, 512, 256, NUM_EXPERTS)
        return {'x': jax.random.normal(k1, (B, T, D), dtype=jnp.float32), 'router_w': jax.random.normal(k2, (D, E), dtype=jnp.float32) * 0.02, 'gate_proj': jax.random.normal(k3, (E, D, F), dtype=jnp.float32) * 0.02, 'up_proj': jax.random.normal(k4, (E, D, F), dtype=jnp.float32) * 0.02, 'down_proj': jax.random.normal(k5, (E, F, D), dtype=jnp.float32) * 0.02}
    _L0_ffn_all = _L0_ffn_setup()
    _L0_ffn_in = {k: v for k, v in _L0_ffn_all.items() if k in ('router_w', 'gate_proj', 'up_proj', 'down_proj')}
    del _L0_ffn_all
    return {'x': x, 'fside_BxS2xS2_0': fside_BxS2xS2_0, 'ctx_1024': ctx_1024, 'L0_ffn_router_w': _L0_ffn_in['router_w'], 'L0_ffn_gate_proj': _L0_ffn_in['gate_proj'], 'L0_ffn_up_proj': _L0_ffn_in['up_proj'], 'L0_ffn_down_proj': _L0_ffn_in['down_proj']}

def reference(x, fside_BxS2xS2_0, ctx_1024, L0_ffn_router_w, L0_ffn_gate_proj, L0_ffn_up_proj, L0_ffn_down_proj):
    import jax
    import jax.numpy as jnp

    def _L0_xattn_ref(x, gate_up_weight, down_weight):
        import jax, jax.numpy as jnp
        import numpy as np
        EPS = 1e-06
        QMAX = 127.0

        def _smooth_quant_linear(x, w):
            amax_x = jnp.max(jnp.abs(x), axis=0)
            amax_w = jnp.max(jnp.abs(w), axis=0)
            s = jnp.sqrt(jnp.maximum(amax_x, EPS) / jnp.maximum(amax_w, EPS))
            s = jnp.maximum(s, EPS)
            xs = x / s
            ws = w * s
            x_scale = jnp.maximum(jnp.max(jnp.abs(xs), axis=-1, keepdims=True), EPS) / QMAX
            w_scale = jnp.maximum(jnp.max(jnp.abs(ws), axis=-1, keepdims=True), EPS) / QMAX
            x_q = jnp.clip(jnp.round(xs / x_scale), -QMAX, QMAX)
            w_q = jnp.clip(jnp.round(ws / w_scale), -QMAX, QMAX)
            return x_q @ w_q.T * x_scale * w_scale.T

        def _expert_forward(xe, guw, dw):
            h = _smooth_quant_linear(xe, guw)
            gate, up = jnp.split(h, 2, axis=-1)
            a = jax.nn.silu(gate) * up
            return _smooth_quant_linear(a, dw)
        return jax.vmap(_expert_forward)(x, gate_up_weight, down_weight)

    def _L0_ffn_ref(x, router_w, gate_proj, up_proj, down_proj):
        import jax, jax.numpy as jnp
        import numpy as np
        NUM_EXPERTS = 8
        EXPERTS_PER_TOK = 2
        E, K = (NUM_EXPERTS, EXPERTS_PER_TOK)
        scores = jnp.einsum('btd,de->bte', x, router_w).astype(jnp.float32)
        routing_weights, routing_idx = jax.lax.top_k(jax.nn.softmax(scores, axis=-1), K)
        routing_weights = (routing_weights / jnp.sum(routing_weights, axis=-1, keepdims=True)).astype(x.dtype)
        onehot = jax.nn.one_hot(routing_idx, E, dtype=x.dtype)
        dispatch_mask = jnp.sum(onehot, axis=2)
        combine_weights = jnp.einsum('btke,btk->bte', onehot, routing_weights)
        dispatched = x[:, :, None, :] * dispatch_mask[..., None]
        gate = jnp.einsum('bted,edf->btef', dispatched, gate_proj)
        up = jnp.einsum('bted,edf->btef', dispatched, up_proj)
        act = jax.nn.silu(gate) * up
        expert_out = jnp.einsum('btef,efd->bted', act, down_proj)
        return jnp.einsum('bted,bte->btd', expert_out, combine_weights)
    x = x + _L0_xattn_ref(_layernorm(x, axis=-1), fside_BxS2xS2_0, ctx_1024)
    x = x + _L0_ffn_ref(_layernorm(x, axis=-1), L0_ffn_router_w, L0_ffn_gate_proj, L0_ffn_up_proj, L0_ffn_down_proj)
    return x

_drawn_inputs = setup_inputs


def setup_inputs(seed=0):
    import zlib

    import numpy as np

    out = dict(_drawn_inputs(seed))
    spreads = {}
    factors = {}
    for name, (base, spread) in spreads.items():
        noise = np.random.default_rng([zlib.crc32(name.encode()), seed]).standard_normal(out[name].shape)
        drawn = base * np.exp(spread * noise) if base else spread * noise
        out[name] = jnp.asarray(drawn.astype(out[name].dtype))
    for name, factor in factors.items():
        out[name] = (out[name] * factor).astype(out[name].dtype)
    return out
```

```python
from contextlib import ExitStack

import concourse.bass as bass
from concourse import mybir

F32 = mybir.dt.float32
F16 = mybir.dt.float16
BF16 = mybir.dt.bfloat16
I32 = mybir.dt.int32
ALU = mybir.AluOpType
ACT = mybir.ActivationFunctionType
AX = mybir.AxisListType

P = 128
LN_EPS = 1e-5
EPS = 1e-6
QMAX = 127.0
ROUND = 12582912.0
X_SCALE = 256.0
A_SCALE = 16.0
C_SCALE = 1024.0


class Signals:

    def __init__(self, nc, ctx):
        self.nc, self.ctx, self.made = nc, ctx, {}

    def __call__(self, name):
        if name not in self.made:
            self.made[name] = self.ctx.enter_context(self.nc.semaphore(name))
        return self.made[name]


class Ring:

    def __init__(self, psum, filled, taken, batches, steps, first, second):
        self.psum, self.filled, self.taken, self.batches = psum, filled, taken, batches
        self.uses = [[u.get(k, 0) for k in range(steps)] for u in (first, second)]
        assert sum(map(sum, self.uses)) % 2 == 0

    def before(self, half, k, u, b):
        first, second = self.uses
        if half == 0 and isinstance(b, int) and b == 0:
            n = sum(first[:k]) + u
            return n, n % 2
        if half == 1 and isinstance(b, int) and b == self.batches - 1:
            n = sum(first) + sum(second[:k]) + u
            one_pass, passes = sum(first) + sum(second), b
        else:
            n = sum(first) + sum(second[:k + 1 if half == 0 else k]) + sum(first[:k]) + u
            one_pass, passes = sum(first) + sum(second), (b - 1 if half == 0 else b)
        return passes * one_pass + n, n % 2

    def fill(self, pe, half, k, u, b):
        n, bank = self.before(half, k, u, b)
        if not (isinstance(n, int) and n < 2):
            pe.wait_ge(self.taken, n - 1)
        return self.psum[:, bank]

    def empty(self, eng, half, k, u, b):
        n, bank = self.before(half, k, u, b)
        eng.wait_ge(self.filled, n + 1)
        return self.psum[:, bank]

    def emptied(self, eng, half, k, u, b):
        eng.wait_ge(self.taken, self.before(half, k, u, b)[0] + 1)


def upto(b, per_batch, j=None):
    return b * per_batch + (per_batch if j is None else j + 1)


def is_first(b):
    return isinstance(b, int) and b == 0


def block_kernel(nc, x, w1, w2, router_w, gate_w, up_w, down_w, out):
    B, T, D = x.shape
    O1 = w1.shape[1]
    I = w2.shape[2]
    E, _, F = gate_w.shape
    J = T // P
    C = D // P
    IC = I // P
    FC = F // P
    NT = B * J
    N = B * T
    TOPK = 2
    TILES = (N * TOPK + E * (P - 1)) // P
    EPB = E // B
    PPB = 3 * EPB
    STEPS = 9
    assert TILES % 2 == 1 and O1 == T == D and 2 * I == O1 and C * F == FC * D

    halves_dram = nc.dram_tensor("token_halves", (N + P, 2 * D), F16).ap()

    with ExitStack() as ctx:
        def sb(name, shape, dt):
            return ctx.enter_context(nc.sbuf_tensor(name, shape, dt))

        def ps(name):
            return ctx.enter_context(nc.psum_tensor(name, [P, 2, 512], F32))

        sem = Signals(nc, ctx)

        gu_hi = sb("gu_hi", [P, E, C, 2 * F], F16)
        gu_lo = sb("gu_lo", [P, E, C, 2 * F], BF16)
        dn_hi = sb("dn_hi", [P, E, FC, D], F16)
        dn_lo = sb("dn_lo", [P, E, FC, D], BF16)
        identf = sb("identf", [P, P], F32)
        identh = sb("identh", [P, P], F16)
        identb = sb("identb", [P, P], BF16)
        below = sb("below", [P, P], BF16)
        onesb = sb("onesb", [P, P], BF16)
        power = sb("power", [P, 2, C], F32)
        rw = sb("rw", [P, C, E], F32)
        scores = sb("scores", [P, NT, E], F32)
        gather_at = sb("gather_at", [P, TILES], I32)
        slot_weight = sb("slot_weight", [P, TILES], F32)
        gu_at = sb("gu_at", [P, TILES], I32)
        dn_at = sb("dn_at", [P, TILES], I32)

        bank_t, bank_r, bank_q, bank_h = ps("bank_t"), ps("bank_r"), ps("bank_q"), ps("bank_h")

        hold_p = sb("hold_p", [P, 1], F32)
        hold_v = sb("hold_v", [P, 1], F32)

        def hold(pool):
            pool.tensor_tensor(hold_p[:], identf[:, 0:1], identf[:, 0:1], ALU.add)

        def spread(ap, shape, axis):
            return ap.unsqueeze(axis).to_broadcast(shape)

        def at(t, b):
            return t[:, b] if isinstance(b, int) else t[:, bass.ds(b, 1)].squeeze(1)

        def row_of(t, b):
            return t[b] if isinstance(b, int) else t[bass.ds(b, 1)].squeeze(0)


        zeros = sb("zeros", [P, D], F32)

        part1 = ExitStack()

        def tmp(name, shape, dt):
            return part1.enter_context(nc.sbuf_tensor(name, shape, dt))

        x_in = tmp("x_in", [P, J, D], F32)
        w1_in = tmp("w1_in", [P, J, D], F32)
        w2_in = tmp("w2_in", [P, J, I], F32)
        xn = tmp("xn", [P, J, D], F32)
        rows1 = tmp("rows1", [P, 3, D], F32)
        h = tmp("h", [P, J, O1], F32)
        xa_q = tmp("xa_q", [P, J, D], BF16)
        wd_q = tmp("wd_q", [P, J, D], BF16)
        xqT = tmp("xqT", [P, C, T], BF16)
        wqT = tmp("wqT", [P, C, O1], BF16)
        av = tmp("av", [P, J, I], F32)
        rows2 = tmp("rows2", [P, 2, I], F32)
        row_w2 = tmp("row_w2", [P, D], F32)
        aqT = tmp("aqT", [P, IC, T], BF16)
        dqT = tmp("dqT", [P, IC, D], BF16)
        x1 = tmp("x1", [P, J, D], F32)
        xn2 = tmp("xn2", [P, J, D], F32)
        halves = tmp("halves", [P, J, 2, D], F16)
        xn2T = tmp("xn2T", [P, 2, D], F32)
        stage = tmp("stage", [P, 2, C * F], F32)
        stats = tmp("stats", [P, 2, J, 6], F32)
        mv = tmp("mv", [P, 2, J, 2], F32)
        rstd = tmp("rstd", [P, 2, J], F32)
        shift = tmp("shift", [P, 2, J], F32)
        amax = [tmp(f"amax{k}", [P, 2, n], F32) for k, n in ((0, C), (1, IC))]
        ratio = [tmp(f"ratio{k}", [P, n], F32) for k, n in ((0, C), (1, IC))]
        smooth = [tmp(f"smooth{k}", [P, 2, n], F32) for k, n in ((0, C), (1, IC))]
        rmax = tmp("rmax", [P, 2, 2, J], F32)
        scale = tmp("scale", [P, 2, 2, J], F32)
        inv = tmp("inv", [P, 2, 2, J], F32)
        a_q, d_q = xa_q[:, :, 0:I], wd_q[:, :, 0:I]

        x_dram = x.rearrange("b (p j) d -> b p j d", j=J)
        out_dram = out[0:N].rearrange("(b p j) d -> b p j d", b=B, j=J)
        halves_out = halves_dram[0:N].rearrange("(b p j) d -> b p (j d)", b=B, j=J)
        w1_dram = w1.rearrange("b (j p) d -> b p j d", p=P)
        w2_dram = w2.rearrange("b (j p) i -> b p j i", p=P)
        expert_dram = (gate_w.rearrange("e (c p) f -> e p c f", p=P), up_w.rearrange("e (c p) f -> e p c f", p=P),
                       down_w.rearrange("e (c p) d -> e p c d", p=P))

        def staged(m):
            return stage[:, m % 2].rearrange("p (c f) -> p c f", c=C if m % 3 < 2 else FC)

        def parts(b, m):
            e = b * EPB + m // 3
            if m % 3 < 2:
                cols = slice(m % 3 * F, (m % 3 + 1) * F)
                return at(gu_hi, e)[:, :, cols], at(gu_lo, e)[:, :, cols]
            return at(dn_hi, e), at(dn_lo, e)

        ring_t = Ring(bank_t, sem("t_filled"), sem("t_taken"), B, STEPS, {0: C, 2: C}, {0: 2 * IC})
        ring_r = Ring(bank_r, sem("r_filled"), sem("r_taken"), B, STEPS, {3: 2, 7: 1}, {2: 2, 6: 1})
        ring_q = Ring(bank_q, sem("q_filled"), sem("q_taken"), B, STEPS, {6: 2, 7: 2}, {5: 1, 6: 1, 8: J + 2})
        ring_h = Ring(bank_h, sem("h_filled"), sem("h_taken"), B, STEPS, {7: J}, {6: J})

        def woven(eng, first, second):
            def run(part, k, b):
                if k in part:
                    part[k](b)

            def both(b):
                for k in range(STEPS):
                    run(second, k, b)
                    run(first, k, b + 1)

            for k in range(STEPS):
                run(first, k, 0)
            both(0)
            with eng.Fori(1, B - 1) as b:
                both(b)
            for k in range(STEPS):
                run(second, k, B - 1)

        block = part1.enter_context(nc.Block())

        @block.sync
        def _(sp):
            sp.dma_start(rw[:], router_w.rearrange("(c p) e -> p c e", p=P)).then_inc(sem("router_in"), 16)

            def load_first(b):
                if not is_first(b):
                    sp.wait_ge(sem("xn_ready"), upto(b, J) - J)
                sp.dma_start(x_in[:], row_of(x_dram, b)).then_inc(sem("x_in"), 16)
                if not is_first(b):
                    sp.wait_ge(sem("wq_ready"), upto(b, 1) - 1)
                sp.dma_start(w1_in[:], row_of(w1_dram, b)).then_inc(sem("w1_in"), 16)

            def load_second(b):
                if not is_first(b):
                    sp.wait_ge(sem("dq_ready"), upto(b, 1) - 1)
                sp.dma_start(w2_in[:], row_of(w2_dram, b)).then_inc(sem("w2_in"), 16)
                if not is_first(b):
                    stored = 16 * (upto(b, 1) - 1)
                    sp.wait_ge(sem("x1_stored"), stored)
                    sp.wait_ge(sem("halves_stored"), stored)
                sp.dma_start(x1[:], row_of(x_dram, b)).then_inc(sem("x_again"), 16)

            def load_experts(b, ms):
                for m in ms:
                    if not (is_first(b) and m < 2):
                        sp.wait_ge(sem("lo_done"), upto(b, PPB, m) - 2)
                    sp.dma_start(staged(m), row_of(expert_dram[m % 3], b * EPB + m // 3)).then_inc(sem(f"stage_in{m % 2}"), 16)

            def store(b):
                sp.wait_ge(sem("x1_ready"), upto(b, J))
                sp.dma_start(row_of(out_dram, b), x1[:]).then_inc(sem("x1_stored"), 16)
                sp.wait_ge(sem("hi_half"), upto(b, 1))
                sp.wait_ge(sem("lo_half"), upto(b, 1))
                sp.dma_start(row_of(halves_out, b), halves[:].rearrange("p j k d -> p (j k d)")).then_inc(sem("halves_stored"), 16)

            woven(sp, {0: load_first}, {0: lambda b: (load_second(b), load_experts(b, range(0, 2))),
                                        2: lambda b: load_experts(b, range(2, 3)),
                                        4: lambda b: load_experts(b, range(3, 4)),
                                        6: lambda b: load_experts(b, range(4, 5)),
                                        7: lambda b: load_experts(b, range(5, 6)), 8: store})
            sp.wait_ge(sem("zeroed"), 1)
            sp.dma_start(out[N:N + P], zeros[:]).then_inc(sem("pad_stored"), 16)
            sp.dma_start(halves_dram[N:N + P], zeros[:].bitcast(F16)).then_inc(sem("pad_stored"), 16)
            sp.wait_ge(sem("pad_stored"), 32)
            sp.wait_ge(sem("router_in"), 16)
            sp.wait_ge(sem("x1_stored"), 16 * B)
            sp.wait_ge(sem("halves_stored"), 16 * B)

        @block.gpsimd
        def _(pool):
            pool.memset(identf[:], 0.0).then_inc(sem("blank"), 1)
            pool.memset(below[:], 1.0).then_inc(sem("blank"), 1)
            pool.memset(power[:, 0], -0.5).then_inc(sem("constants"), 1)
            pool.memset(power[:, 1], 0.5).then_inc(sem("constants"), 1)
            pool.wait_ge(sem("blank"), 2)
            pool.affine_select(out=identf[:], in_=identf[:], compare_op=ALU.not_equal, fill=1.0, base=0,
                               pattern=[[-1, P]], channel_multiplier=1).then_inc(sem("constants"), 1)
            pool.affine_select(out=below[:], in_=below[:], compare_op=ALU.is_gt, fill=0.0, base=0,
                               pattern=[[1, P]], channel_multiplier=-1).then_inc(sem("constants"), 1)
            pool.wait_ge(sem("constants"), 4)
            pool.tensor_copy(identb[:], identf[:]).then_inc(sem("idents"), 1)
            pool.tensor_copy(identh[:], identf[:]).then_inc(sem("idents"), 1)
            pool.memset(onesb[:], 1.0).then_inc(sem("constants"), 1)
            pool.memset(zeros[:], 0.0).then_inc(sem("zeroed"), 1)

            def split(b, ms):
                for m in ms:
                    hi, lo = parts(b, m)
                    pool.wait_ge(sem("hi_done"), upto(b, PPB, m))
                    pool.tensor_tensor(lo, staged(m), hi, ALU.subtract).then_inc(sem("lo_done"), 1)

            def root(out_ap, in_ap, which, ready, done, b):
                pool.wait_ge(ready, upto(b, 1))
                pool.tensor_tensor(out_ap, in_ap, power[:, which, 0:in_ap.shape[1]], ALU.pow).then_inc(done, 1)

            def first1(b):
                root(rstd[:, 0], mv[:, 0, :, 1], 0, sem("var0"), sem("rstd0"), b)

            def first3(b):
                root(smooth[0][:, 1], ratio[0][:], 1, sem("ratio0"), sem("root0"), b)

            def first4(b):
                ring_r.emptied(pool, 0, 3, 1, b)
                pool.tensor_tensor(w1_in[:], w1_in[:], spread(rows1[:, 1], [P, J, D], 1), ALU.mult).then_inc(sem("ws_ready"), 1)

            def first6(b):
                pool.wait_ge(sem("wq_up"), upto(b, 1))
                if not is_first(b):
                    pool.wait_ge(ring_q.filled, ring_q.before(1, 6, 0, b - 1)[0] + 1)
                hold(pool)
                pool.tensor_scalar(wd_q[:], w1_in[:], ROUND, None, ALU.subtract).then_inc(sem("wq_ready"), 1)

            def second2(b):
                root(smooth[1][:, 1], ratio[1][:], 1, sem("ratio1"), sem("root1"), b)

            def second3(b):
                ring_r.emptied(pool, 1, 2, 1, b)
                pool.tensor_tensor(w2_in[:], w2_in[:], spread(rows2[:, 1], [P, J, I], 1), ALU.mult).then_inc(sem("ds_ready"), 1)

            def second5(b):
                pool.wait_ge(sem("dq_up"), upto(b, 1))
                hold(pool)
                pool.tensor_scalar(d_q, w2_in[:], ROUND, None, ALU.subtract).then_inc(sem("dq_ready"), 1)

            def second7(b):
                pool.wait_ge(sem("x_again"), 16 * upto(b, 1))
                for j in range(J):
                    ring_h.emptied(pool, 1, 6, j, b)
                    pool.tensor_tensor(x1[:, j], x1[:, j], xn2[:, j], ALU.add).then_inc(sem("x1_ready"), 1)

            def second8(b):
                root(rstd[:, 1], mv[:, 1, :, 1], 0, sem("var1"), sem("rstd1"), b)
                split(b, range(5, 6))
                pool.wait_ge(sem("xn2_ready"), upto(b, J))
                pool.wait_ge(sem("hi_half"), upto(b, 1))
                if not is_first(b):
                    pool.wait_ge(sem("halves_stored"), 16 * (upto(b, 1) - 1))
                pool.tensor_tensor(halves[:, :, 1], xn2[:], halves[:, :, 0], ALU.subtract).then_inc(sem("lo_half"), 1)

            woven(pool, {1: first1, 3: first3, 4: first4, 6: first6},
                  {0: lambda b: split(b, range(0, 1)), 1: lambda b: split(b, range(1, 2)), 2: second2,
                   3: second3, 4: lambda b: split(b, range(2, 3)), 5: second5, 6: lambda b: split(b, range(3, 5)),
                   7: second7, 8: second8})

        @block.vector
        def _(dve):
            def layernorm_stats(b, which, src):
                for j in range(J):
                    dve.bn_stats(stats[:, which, j], src[:, j]).then_inc(sem(f"stats{which}"), 1)
                dve.wait_ge(sem(f"stats{which}"), upto(b, J))
                dve.tensor_copy(hold_v[:], stats[:, which, 0, 0:1])
                for j in range(J):
                    dve.bn_aggr(mv[:, which, j], stats[:, which, j]).then_inc(sem(f"moments{which}"), 1)
                dve.wait_ge(sem(f"moments{which}"), upto(b, J))
                dve.tensor_scalar(mv[:, which, :, 1], mv[:, which, :, 1], LN_EPS, None, ALU.add).then_inc(sem(f"var{which}"), 1)

            def layernorm_shift(b, which):
                dve.scalar_tensor_tensor(out=shift[:, which], in0=mv[:, which, :, 0], scalar=-1.0, in1=rstd[:, which],
                                         op0=ALU.mult, op1=ALU.mult).then_inc(sem(f"shift{which}"), 1)

            def column_max(b, half, k, use, dst, chunks):
                for c in range(chunks):
                    bank = ring_t.empty(dve, half, k, use + c, b)
                    dve.tensor_reduce(dst[:, c:c + 1], bank, AX.X, ALU.max,
                                      apply_absolute_value=True).then_inc(ring_t.taken, 1)

            def smoothing(b, half, last):
                done = sem(f"clamped{half}")
                ring_t.emptied(dve, half, *last, b)
                dve.tensor_scalar(amax[half][:], amax[half][:], EPS, None, ALU.max).then_inc(done, 1)
                dve.wait_ge(done, upto(b, 2, 0))
                dve.reciprocal(ratio[half][:], amax[half][:, 1]).then_inc(done, 1)
                dve.wait_ge(done, upto(b, 2, 1))
                dve.tensor_tensor(ratio[half][:], ratio[half][:], amax[half][:, 0], ALU.mult).then_inc(sem(f"ratio{half}"), 1)

            def smoothing_end(b, half):
                done = sem(f"smooth{half}")
                dve.wait_ge(sem(f"root{half}"), upto(b, 1))
                dve.tensor_scalar(smooth[half][:, 1], smooth[half][:, 1], EPS, None, ALU.max).then_inc(done, 1)
                dve.wait_ge(done, upto(b, 2, 0))
                dve.reciprocal(smooth[half][:, 0], smooth[half][:, 1]).then_inc(done, 1)

            def row_scales(b, half, side, src, ready):
                done = sem(f"row_max{half}{side}")
                dve.wait_ge(ready, upto(b, 1))
                dve.tensor_reduce(rmax[:, half, side], src, AX.X, ALU.max, apply_absolute_value=True).then_inc(done, 1)
                dve.wait_ge(done, upto(b, 2, 0))
                dve.tensor_scalar(scale[:, half, side], rmax[:, half, side], EPS, 1.0 / QMAX, ALU.max,
                                  ALU.mult).then_inc(done, 1)
                dve.wait_ge(done, upto(b, 2, 1))
                dve.reciprocal(inv[:, half, side], scale[:, half, side]).then_inc(sem(f"inv{half}{side}"), 1)

            def first0(b):
                dve.wait_ge(sem("x_in"), 16 * upto(b, 1))
                layernorm_stats(b, 0, x_in)

            def first1(b):
                dve.wait_ge(sem("rstd0"), upto(b, 1))
                layernorm_shift(b, 0)
                column_max(b, 0, 0, 0, amax[0][:, 1], C)

            def first2(b):
                column_max(b, 0, 2, 0, amax[0][:, 0], C)
                smoothing(b, 0, (2, C - 1))

            def first3(b):
                smoothing_end(b, 0)

            def first4(b):
                ring_r.emptied(dve, 0, 3, 0, b)
                dve.tensor_tensor(xn[:], xn[:], spread(rows1[:, 0], [P, J, D], 1), ALU.mult).then_inc(sem("xs_ready"), 1)
                row_scales(b, 0, 0, xn[:], sem("xs_ready"))

            def first5(b):
                row_scales(b, 0, 1, w1_in[:], sem("ws_ready"))

            def first6(b):
                dve.wait_ge(sem("xq_up"), upto(b, 1))
                if not is_first(b):
                    dve.wait_ge(ring_q.filled, ring_q.before(1, 5, 0, b - 1)[0] + 1)
                dve.tensor_scalar(xa_q[:], xn[:], ROUND, None, ALU.subtract).then_inc(sem("xq_ready"), 1)

            def first7(b):
                ring_r.emptied(dve, 0, 7, 0, b)
                if not is_first(b):
                    dve.wait_ge(sem("silu_done"), upto(b, 1) - 1)
                for j in range(J):
                    bank = ring_h.empty(dve, 0, 7, j, b)
                    dve.scalar_tensor_tensor(out=h[:, j], in0=bank, scalar=scale[:, 0, 0, j:j + 1], in1=rows1[:, 2],
                                             op0=ALU.mult, op1=ALU.mult).then_inc(ring_h.taken, 1)

            def second0(b):
                dve.wait_ge(sem("silu_done"), upto(b, 1))
                dve.tensor_tensor(av[:], av[:], h[:, :, I:2 * I], ALU.mult).then_inc(sem("a_ready"), 1)

            def second1(b):
                column_max(b, 1, 0, 0, amax[1][:, 1], IC)
                column_max(b, 1, 0, IC, amax[1][:, 0], IC)
                smoothing(b, 1, (0, 2 * IC - 1))

            def second2(b):
                smoothing_end(b, 1)

            def second3(b):
                ring_r.emptied(dve, 1, 2, 0, b)
                dve.tensor_tensor(av[:], av[:], spread(rows2[:, 0], [P, J, I], 1), ALU.mult).then_inc(sem("as_ready"), 1)
                row_scales(b, 1, 0, av[:], sem("as_ready"))

            def second4(b):
                row_scales(b, 1, 1, w2_in[:], sem("ds_ready"))

            def second5(b):
                dve.wait_ge(sem("aq_up"), upto(b, 1))
                dve.tensor_scalar(a_q, av[:], ROUND, None, ALU.subtract).then_inc(sem("aq_ready"), 1)

            def second6(b):
                ring_r.emptied(dve, 1, 6, 0, b)
                if not is_first(b):
                    dve.wait_ge(sem("lo_half"), upto(b, 1) - 1)
                    ring_q.emptied(dve, 1, 8, 4, b - 1)
                for j in range(J):
                    bank = ring_h.empty(dve, 1, 6, j, b)
                    dve.scalar_tensor_tensor(out=xn2[:, j], in0=bank, scalar=scale[:, 1, 0, j:j + 1], in1=row_w2[:],
                                             op0=ALU.mult, op1=ALU.mult).then_inc(ring_h.taken, 1)

            def second7(b):
                dve.wait_ge(sem("x1_ready"), upto(b, J))
                layernorm_stats(b, 1, x1)

            def second8(b):
                dve.wait_ge(sem("rstd1"), upto(b, 1))
                dve.tensor_scalar(rstd[:, 1], rstd[:, 1], X_SCALE, None, ALU.mult).then_inc(sem("rstd1_scaled"), 1)
                dve.wait_ge(sem("rstd1_scaled"), upto(b, 1))
                layernorm_shift(b, 1)

            woven(dve, {0: first0, 1: first1, 2: first2, 3: first3, 4: first4, 5: first5, 6: first6, 7: first7},
                  {0: second0, 1: second1, 2: second2, 3: second3, 4: second4, 5: second5, 6: second6,
                   7: second7, 8: second8})

        @block.scalar
        def _(act):
            def normalise(b, which, src, dst, done):
                act.wait_ge(sem(f"shift{which}"), upto(b, 1))
                for j in range(J):
                    act.activation(dst[:, j], src[:, j], ACT.Identity, bias=shift[:, which, j:j + 1],
                                   scale=rstd[:, which, j:j + 1]).then_inc(done, 1)

            def take_row(half, k, u, b, dst):
                bank = ring_r.empty(act, half, k, u, b)
                act.activation(dst, bank[:, 0:dst.shape[1]], ACT.Copy).then_inc(ring_r.taken, 1)

            def scale_up(b, half, side, t, done):
                act.wait_ge(sem(f"inv{half}{side}"), upto(b, 1))
                for j in range(J):
                    ins = act.activation(t[:, j], t[:, j], ACT.Identity, bias=ROUND, scale=inv[:, half, side, j:j + 1])
                ins.then_inc(done, 1)

            def take_transposed(half, k, u, b, dst):
                bank = ring_q.empty(act, half, k, u, b)
                act.activation(dst, bank.bitcast(BF16).rearrange("p (c t) -> p c t", c=2), ACT.Copy).then_inc(ring_q.taken, 1)

            def highs(b, ms):
                for m in ms:
                    hi, _ = parts(b, m)
                    act.wait_ge(sem(f"stage_in{m % 2}"), 16 * upto(b, PPB // 2, m // 2))
                    act.activation(hi, staged(m), ACT.Copy).then_inc(sem("hi_done"), 1)

            def first1(b):
                if not is_first(b):
                    act.wait_ge(sem("xq_ready"), upto(b, 1) - 1)
                normalise(b, 0, x_in, xn, sem("xn_ready"))

            def first3(b):
                if not is_first(b):
                    act.wait_ge(sem("xs_ready"), upto(b, 1) - 1)
                    act.wait_ge(sem("ws_ready"), upto(b, 1) - 1)
                take_row(0, 3, 0, b, rows1[:, 0])
                take_row(0, 3, 1, b, rows1[:, 1])

            def first5(b):
                scale_up(b, 0, 0, xn, sem("xq_up"))

            def first6(b):
                scale_up(b, 0, 1, w1_in, sem("wq_up"))
                if not is_first(b):
                    act.wait_ge(ring_h.filled, ring_h.before(0, 7, J - 1, b - 1)[0] + 1)
                for u in range(2):
                    take_transposed(0, 6, u, b, xqT[:, 2 * u:2 * u + 2])

            def first7(b):
                for u in range(2):
                    take_transposed(0, 7, u, b, wqT[:, 2 * u:2 * u + 2])
                if not is_first(b):
                    ring_h.emptied(act, 0, 7, J - 1, b - 1)
                take_row(0, 7, 0, b, rows1[:, 2])

            def second0(b):
                if not is_first(b):
                    act.wait_ge(sem("aq_ready"), upto(b, 1) - 1)
                ring_h.emptied(act, 0, 7, J - 1, b)
                act.activation(av[:], h[:, :, 0:I], ACT.Silu).then_inc(sem("silu_done"), 1)
                highs(b, range(0, 2))

            def second2(b):
                if not is_first(b):
                    act.wait_ge(sem("as_ready"), upto(b, 1) - 1)
                    act.wait_ge(sem("ds_ready"), upto(b, 1) - 1)
                take_row(1, 2, 0, b, rows2[:, 0])
                take_row(1, 2, 1, b, rows2[:, 1])

            def second4(b):
                scale_up(b, 1, 0, av, sem("aq_up"))
                highs(b, range(2, 3))

            def second5(b):
                scale_up(b, 1, 1, w2_in, sem("dq_up"))
                if not is_first(b):
                    act.wait_ge(ring_h.filled, ring_h.before(1, 6, J - 1, b - 1)[0] + 1)
                take_transposed(1, 5, 0, b, aqT[:])

            def second6(b):
                take_transposed(1, 6, 0, b, dqT[:])
                if not is_first(b):
                    ring_h.emptied(act, 1, 6, J - 1, b - 1)
                take_row(1, 6, 0, b, row_w2[:])
                highs(b, range(3, 5))

            def second8(b):
                highs(b, range(5, 6))
                normalise(b, 1, x1, xn2, sem("xn2_ready"))
                act.wait_ge(sem("xn2_ready"), upto(b, J))
                if not is_first(b):
                    act.wait_ge(sem("halves_stored"), 16 * (upto(b, 1) - 1))
                act.activation(halves[:, :, 0], xn2[:], ACT.Copy).then_inc(sem("hi_half"), 1)
                for half in range(J // 2):
                    for j in range(2):
                        bank = ring_q.empty(act, 1, 8, 3 * half + j, b)
                        act.activation(xn2T[:, j], bank, ACT.Copy).then_inc(ring_q.taken, 1)
                    bank = ring_q.empty(act, 1, 8, 3 * half + 2, b)
                    tile = b * J + 2 * half
                    dst = scores[:, tile:tile + 2] if isinstance(b, int) else scores[:, bass.ds(tile, 2)]
                    act.activation(dst, bank[:, 0:2 * E].rearrange("p (j e) -> p j e", e=E), ACT.Copy,
                                   scale=1.0 / X_SCALE).then_inc(ring_q.taken, 1)

            woven(act, {1: first1, 3: first3, 5: first5, 6: first6, 7: first7},
                  {0: second0, 2: second2, 4: second4, 5: second5, 6: second6, 8: second8})

        @block.tensor
        def _(pe):
            pe.wait_ge(sem("idents"), 2)
            pe.wait_ge(sem("router_in"), 16)

            def transpose_columns(half, k, use, b, src, chunks):
                for c in range(chunks):
                    bank = ring_t.fill(pe, half, k, use + c, b)
                    for j in range(J):
                        ins = pe.transpose(bank[:, j * P:(j + 1) * P], src[:, j, c * P:(c + 1) * P], identf[:])
                    ins.then_inc(ring_t.filled, 1)

            def transpose_quantised(half, k, use, b, src, chunks):
                for u in range(chunks // 2):
                    bank = ring_q.fill(pe, half, k, use + u, b).bitcast(BF16)
                    for c in range(2):
                        for j in range(J):
                            ins = pe.transpose(bank[:, (c * J + j) * P:(c * J + j + 1) * P],
                                               src[:, j, (2 * u + c) * P:(2 * u + c + 1) * P], identb[:])
                    ins.then_inc(ring_q.filled, 1)

            def as_row(half, k, u, b, columns):
                bank = ring_r.fill(pe, half, k, u, b)
                n = columns.shape[1]
                for c in range(n):
                    ins = pe.matmul(bank[:, c * P:(c + 1) * P], columns[:, c:c + 1].to_broadcast([P, P]), identf[:],
                                    start=True, stop=True)
                ins.then_inc(ring_r.filled, 1)

            def product(half, k, b, lhs, rhs, chunks):
                for j in range(J):
                    bank = ring_h.fill(pe, half, k, j, b)
                    for c in range(chunks):
                        ins = pe.matmul(bank, lhs[:, c, j * P:(j + 1) * P], rhs[:, c], start=(c == 0), stop=(c == chunks - 1))
                    ins.then_inc(ring_h.filled, 1)

            def first0(b):
                pe.wait_ge(sem("w1_in"), 16 * upto(b, 1))
                transpose_columns(0, 0, 0, b, w1_in, C)

            def first2(b):
                pe.wait_ge(sem("xn_ready"), upto(b, J))
                transpose_columns(0, 2, 0, b, xn, C)

            def first3(b):
                pe.wait_ge(sem("smooth0"), upto(b, 2))
                as_row(0, 3, 0, b, smooth[0][:, 0])
                as_row(0, 3, 1, b, smooth[0][:, 1])

            def first6(b):
                pe.wait_ge(sem("xq_ready"), upto(b, 1))
                transpose_quantised(0, 6, 0, b, xa_q, C)

            def first7(b):
                pe.wait_ge(sem("wq_ready"), upto(b, 1))
                transpose_quantised(0, 7, 0, b, wd_q, C)
                pe.wait_ge(sem("inv01"), upto(b, 1))
                as_row(0, 7, 0, b, scale[:, 0, 1])
                ring_q.emptied(pe, 0, 7, 1, b)
                product(0, 7, b, xqT, wqT, C)

            def second0(b):
                pe.wait_ge(sem("w2_in"), 16 * upto(b, 1))
                transpose_columns(1, 0, 0, b, w2_in, IC)
                pe.wait_ge(sem("a_ready"), upto(b, 1))
                transpose_columns(1, 0, IC, b, av, IC)

            def second2(b):
                pe.wait_ge(sem("smooth1"), upto(b, 2))
                as_row(1, 2, 0, b, smooth[1][:, 0])
                as_row(1, 2, 1, b, smooth[1][:, 1])

            def second5(b):
                pe.wait_ge(sem("aq_ready"), upto(b, 1))
                transpose_quantised(1, 5, 0, b, a_q, IC)

            def second6(b):
                pe.wait_ge(sem("dq_ready"), upto(b, 1))
                transpose_quantised(1, 6, 0, b, d_q, IC)
                pe.wait_ge(sem("inv11"), upto(b, 1))
                as_row(1, 6, 0, b, scale[:, 1, 1])
                ring_q.emptied(pe, 1, 6, 0, b)
                product(1, 6, b, aqT, dqT, IC)

            def second8(b):
                for half in range(J // 2):
                    pe.wait_ge(sem("xn2_ready"), upto(b, J, 2 * half + 1))
                    for j in range(2):
                        bank = ring_q.fill(pe, 1, 8, 3 * half + j, b)
                        for c in range(C):
                            ins = pe.transpose(bank[:, c * P:(c + 1) * P], xn2[:, 2 * half + j, c * P:(c + 1) * P], identf[:])
                        ins.then_inc(ring_q.filled, 1)
                    ring_q.emptied(pe, 1, 8, 3 * half + 1, b)
                    bank = ring_q.fill(pe, 1, 8, 3 * half + 2, b)
                    for j in range(2):
                        for c in range(C):
                            ins = pe.matmul(bank[:, j * E:(j + 1) * E], xn2T[:, j, c * P:(c + 1) * P], rw[:, c],
                                            start=(c == 0), stop=(c == C - 1))
                    ins.then_inc(ring_q.filled, 1)

            woven(pe, {0: first0, 2: first2, 3: first3, 6: first6, 7: first7},
                  {0: second0, 2: second2, 5: second5, 6: second6, 8: second8})

        part1.close()

        K = TOPK

        def buf(name, shape, dt=F32):
            return ctx.enter_context(nc.sbuf_tensor(name, shape, dt))

        lane = buf("lane", [P, P])
        preference = buf("preference", [P, E])
        token = buf("token", [P, NT])
        pad_row = buf("pad_row", [P, 1])
        prob = buf("prob", [P, NT, E])
        work = buf("work", [P, NT, E])
        best = buf("best", [P, K, NT])
        pick = buf("pick", [P, K, NT])
        chosen = buf("chosen", [P, K, NT, E])
        mask = buf("mask", [P, NT, E], BF16)
        run_a = buf("run_a", [P, NT, E])
        run_b = buf("run_b", [P, NT, E])
        total = buf("total", [P, NT])
        ends = [buf(f"ends{i}", [P, E]) for i in range(2)]
        count = buf("count", [P, E])
        slot = buf("slot", [P, NT, E])
        pos = buf("pos", [P, K, NT])
        tile_of = buf("tile_of", [P, K, NT])
        lane_of = buf("lane_of", [P, K, NT])
        weight = buf("weight", [P, K, NT])
        weight_hi = buf("weight_hi", [P, K, NT], F16)
        weight_lo = buf("weight_lo", [P, K, NT])
        in_lane = buf("in_lane", [P, K * NT, P], F16)
        in_tile = buf("in_tile", [P, K * NT, TILES])
        packed = buf("packed", [P, K * NT, 3, TILES], F16)
        expert_of = buf("expert_of", [P, TILES])
        ended = buf("ended", [P, TILES, E])
        unused = buf("unused", [P, TILES])
        table = buf("table", [P, 3 * TILES])
        gather_idx = [buf(f"gather_idx{k}", [P, 1], I32) for k in range(2)]
        scatter_idx = [buf(f"scatter_idx{k}", [P, 1], I32) for k in range(2)]
        xg = [buf(f"xg{k}", [P, 2 * D], F16) for k in range(2)]
        xT = [buf(f"xT{k}", [P, 2, C, P], F16) for k in range(2)]
        gated = [buf(f"gated{k}", [P, F]) for k in range(2)]
        act_hl = [buf(f"act_hl{k}", [P, 2, F], F16) for k in range(2)]
        aT = [buf(f"aT{k}", [P, 2, FC, P], F16) for k in range(2)]
        y = [buf(f"y{k}", [P, D]) for k in range(2)]

        bank_x, bank_gu, bank_a, bank_y = bank_t, bank_r, bank_q, bank_h
        gu_hi_at, gu_lo_at = (t[:].rearrange("p e c f -> p (e c f)") for t in (gu_hi, gu_lo))
        dn_hi_at, dn_lo_at = (t[:].rearrange("p e c d -> p (e c d)") for t in (dn_hi, dn_lo))
        acc_rows = out
        LAST = TILES - 1

        class Tile:

            def __init__(self, m, k):
                self.parity, self.half, self.i = k % 2, m + k // 2, 2 * m + k
                self.number = self.i if isinstance(self.i, int) else None

            def column(self, t):
                return t[:, self.i:self.i + 1] if self.number is not None else t[:, bass.ds(self.i, 1)]

        def over_tiles(eng, step):
            for k in range(3):
                step(0, k)
            with eng.Fori(1, (TILES - 3) // 2) as m:
                step(m, 1)
                step(m, 2)
            step(0, TILES - 2)
            step(0, TILES - 1)

        block = ctx.enter_context(nc.Block())

        @block.gpsimd
        def _(pool):
            pool.iota(lane[:], [[1, P]], base=0, channel_multiplier=0, allow_small_or_imprecise_dtypes=True).then_inc(sem("numbers"), 1)
            pool.iota(preference[:], [[-1, E]], base=E, channel_multiplier=0, allow_small_or_imprecise_dtypes=True).then_inc(sem("numbers"), 1)
            pool.iota(token[:].rearrange("p (b j) -> p b j", b=B), [[T, B], [1, J]], base=1, channel_multiplier=J,
                      allow_small_or_imprecise_dtypes=True).then_inc(sem("numbers"), 1)
            pool.iota(pad_row[:], [[0, 1]], base=N + 1, channel_multiplier=1, allow_small_or_imprecise_dtypes=True).then_inc(sem("numbers"), 1)

            def gather(m, k):
                t = Tile(m, k)
                if not (t.number is not None and t.number < 2):
                    pool.wait_ge(sem("x_filled"), t.i - 1)
                pool.tensor_copy(gather_idx[t.parity][:], t.column(gather_at)).then_inc(sem("gather_idx"), 1)
                pool.wait_ge(sem("gather_idx"), t.i + 1)
                hold(pool)
                pool.indirect_dma_start(out=xg[t.parity][:], out_offset=None, in_=halves_dram,
                                        in_offset=bass.IndirectOffsetOnAxis(ap=gather_idx[t.parity][:, 0:1], axis=0)
                                        ).then_inc(sem(f"gathered{t.parity}"), 16)

            def scatter(m, k):
                t = Tile(m, k)
                pool.tensor_copy(scatter_idx[t.parity][:], t.column(gather_at)).then_inc(sem("scatter_idx"), 1)
                pool.wait_ge(sem("scatter_idx"), t.i + 1)
                pool.wait_ge(sem("y_taken"), t.i + 1)
                if t.number != 0:
                    pool.wait_ge(sem("added"), 16 * t.i)
                hold(pool)
                pool.indirect_dma_start(out=acc_rows, out_offset=bass.IndirectOffsetOnAxis(ap=scatter_idx[t.parity][:, 0:1], axis=0),
                                        in_=y[t.parity][:], in_offset=None, compute_op=ALU.add).then_inc(sem("added"), 16)

            pool.wait_ge(sem("gather_ready"), 1)
            for k in range(3):
                gather(0, k)
            def step(m, k):
                t = Tile(m, k)
                if t.number is None or t.number + 3 < TILES:
                    gather(m, k + 3)
                if t.number != 0:
                    scatter(m, k - 1)
            for k in range(3):
                step(0, k)
            with pool.Fori(1, (TILES - 5) // 2) as m:
                step(m, 1)
                step(m, 2)
            for k in range(TILES - 4, TILES):
                step(0, k)
            scatter(0, LAST)
            pool.wait_ge(sem("added"), 16 * TILES)

        @block.vector
        def _(dve):
            steps = [0]

            def then(ins):
                steps[0] += 1
                ins.then_inc(sem("route"), 1)
                dve.wait_ge(sem("route"), steps[0])

            shape = [P, NT, E]
            dve.wait_ge(sem("numbers"), 4)
            then(dve.tensor_reduce(total[:], scores[:], AX.X, ALU.max))
            dve.tensor_tensor(work[:], scores[:], spread(total[:], shape, 2), ALU.subtract).then_inc(sem("shifted"), 1)
            dve.wait_ge(sem("exp_done"), 1)
            then(dve.tensor_reduce(total[:], prob[:], AX.X, ALU.add))
            then(dve.reciprocal(total[:], total[:]))
            then(dve.tensor_tensor(prob[:], prob[:], spread(total[:], shape, 2), ALU.mult))
            for k in range(K):
                then(dve.tensor_reduce(best[:, k], prob[:], AX.X, ALU.max))
                then(dve.tensor_tensor(work[:], prob[:], spread(best[:, k], shape, 2), ALU.is_equal))
                then(dve.tensor_tensor(work[:], work[:], spread(preference[:], shape, 1), ALU.mult))
                then(dve.tensor_reduce(pick[:, k], work[:], AX.X, ALU.max))
                then(dve.tensor_tensor(chosen[:, k], spread(preference[:], shape, 1), spread(pick[:, k], shape, 2), ALU.is_equal))
                if k == 0:
                    then(dve.scalar_tensor_tensor(out=prob[:], in0=chosen[:, 0], scalar=-2.0, in1=prob[:], op0=ALU.mult, op1=ALU.add))
            dve.tensor_tensor(mask[:], chosen[:, 0], chosen[:, 1], ALU.add).then_inc(sem("mask_ready"), 1)
            then(dve.tensor_tensor(total[:], best[:, 0], best[:, 1], ALU.add))
            then(dve.reciprocal(total[:], total[:]))
            then(dve.tensor_scalar(total[:], total[:], C_SCALE, None, ALU.mult))
            then(dve.tensor_tensor(weight[:], best[:], spread(total[:], [P, K, NT], 1), ALU.mult))
            then(dve.tensor_copy(weight_hi[:], weight[:]))
            then(dve.tensor_tensor(weight_lo[:], weight[:], weight_hi[:], ALU.subtract))
            dve.wait_ge(sem("ranked"), 1)
            then(dve.tensor_copy(run_a[:].rearrange("p t e -> p (t e)"), bank_r[:, 1, 0:NT * E]))
            then(dve.tensor_copy(slot[:].rearrange("p t e -> p (t e)"), bank_r[:, 0, 0:NT * E]))
            then(dve.tensor_tensor(slot[:], slot[:], run_a[:], ALU.subtract))
            a, b2 = run_a, run_b
            step = 1
            while step < NT:
                dve.tensor_copy(b2[:, 0:step], a[:, 0:step])
                then(dve.tensor_tensor(b2[:, step:], a[:, step:], a[:, :NT - step], ALU.add))
                a, b2, step = b2, a, 2 * step
            then(dve.tensor_scalar(count[:], a[:, NT - 1], 1.0 / P, 0.5 - 0.5 / P, ALU.mult, ALU.add))
            then(dve.tensor_scalar(count[:], count[:], ROUND, ROUND, ALU.add, ALU.subtract))
            then(dve.tensor_copy(ends[0][:], count[:]))
            c, d, step = ends[0], ends[1], 1
            while step < E:
                dve.tensor_copy(d[:, 0:step], c[:, 0:step])
                then(dve.tensor_tensor(d[:, step:], c[:, step:], c[:, :E - step], ALU.add))
                c, d, step = d, c, 2 * step
            then(dve.tensor_tensor(count[:], c[:], count[:], ALU.subtract))
            then(dve.tensor_scalar(count[:], count[:], float(P), None, ALU.mult))
            then(dve.tensor_tensor(slot[:], slot[:], a[:], ALU.add))
            then(dve.tensor_tensor(slot[:], slot[:], spread(count[:], shape, 1), ALU.add))
            for k in range(K):
                then(dve.tensor_tensor(work[:], chosen[:, k], slot[:], ALU.mult))
                then(dve.tensor_reduce(pos[:, k], work[:], AX.X, ALU.add))
            then(dve.tensor_scalar(tile_of[:], pos[:], 1.0 / P, 0.5 / P - 0.5, ALU.mult, ALU.add))
            then(dve.tensor_scalar(tile_of[:], tile_of[:], ROUND, ROUND, ALU.add, ALU.subtract))
            then(dve.scalar_tensor_tensor(out=lane_of[:], in0=tile_of[:], scalar=-float(P), in1=pos[:], op0=ALU.mult, op1=ALU.add))
            flat = lambda t: t[:].rearrange("p k t -> p (k t)")
            dve.tensor_tensor(in_lane[:], spread(lane[:], [P, K * NT, P], 1), spread(flat(lane_of), [P, K * NT, P], 2), ALU.is_equal)
            then(dve.tensor_tensor(in_tile[:], spread(lane[:, 0:TILES], [P, K * NT, TILES], 1),
                                   spread(flat(tile_of), [P, K * NT, TILES], 2), ALU.is_equal))
            for k in range(K):
                half = slice(k * NT, (k + 1) * NT)
                dve.tensor_tensor(packed[:, half, 0], in_tile[:, half], spread(token[:], [P, NT, TILES], 2), ALU.mult)
            dve.tensor_tensor(packed[:, :, 1], in_tile[:], spread(flat(weight_hi), [P, K * NT, TILES], 2), ALU.mult)
            dve.tensor_tensor(packed[:, :, 2], in_tile[:], spread(flat(weight_lo), [P, K * NT, TILES], 2),
                              ALU.mult).then_inc(sem("packed"), 1)
            then(dve.tensor_tensor(ended[:], spread(c[:], [P, TILES, E], 1), spread(lane[:, 0:TILES], [P, TILES, E], 2), ALU.is_le))
            then(dve.tensor_reduce(expert_of[:], ended[:], AX.X, ALU.add))
            then(dve.tensor_scalar(expert_of[:], expert_of[:], float(E - 1), None, ALU.min))
            dve.tensor_scalar(gu_at[:], expert_of[:], float(C * 2 * F), None, ALU.mult).then_inc(sem("experts_known"), 1)
            dve.tensor_scalar(dn_at[:], expert_of[:], float(FC * D), None, ALU.mult).then_inc(sem("experts_known"), 1)
            dve.wait_ge(sem("sorted"), 1)
            then(dve.tensor_copy(table[:], bank_y[:, 0, 0:3 * TILES]))
            then(dve.tensor_scalar(unused[:], table[:, 0:TILES], 0.0, pad_row[:, 0:1], ALU.is_equal, ALU.mult))
            dve.scalar_tensor_tensor(out=gather_at[:], in0=table[:, 0:TILES], scalar=-1.0, in1=unused[:], op0=ALU.add,
                                     op1=ALU.add).then_inc(sem("gather_ready"), 1)
            then(dve.tensor_tensor(slot_weight[:], table[:, TILES:2 * TILES], table[:, 2 * TILES:], ALU.add))
            dve.tensor_scalar(slot_weight[:], slot_weight[:], 1.0 / (C_SCALE * A_SCALE), None, ALU.mult).then_inc(sem("weights_ready"), 1)

            def take_x(m, k):
                t = Tile(m, k)
                dve.wait_ge(sem("x_filled"), t.i + 1)
                if not (t.number is not None and t.number < 2):
                    dve.wait_ge(sem("gu_filled"), t.i - 1)
                dve.tensor_copy(xT[t.parity][:].rearrange("p h c t -> p (h c t)"),
                                bank_x[:, t.parity].bitcast(F16)).then_inc(sem("x_taken"), 1)

            def activate(m, k):
                t = Tile(m, k)
                dve.wait_ge(sem("gated"), t.i + 1)
                dve.scalar_tensor_tensor(out=gated[t.parity][:], in0=bank_gu[:, t.parity, F:2 * F], scalar=A_SCALE / X_SCALE,
                                         in1=gated[t.parity][:], op0=ALU.mult, op1=ALU.mult).then_inc(sem("gu_taken"), 1)
                dve.wait_ge(sem("act_hi"), t.i + 1)
                dve.tensor_tensor(act_hl[t.parity][:, 1], gated[t.parity][:], act_hl[t.parity][:, 0],
                                  ALU.subtract).then_inc(sem("act_lo"), 1)

            def step(m, k):
                t = Tile(m, k)
                if t.number != 0:
                    activate(m, k - 1)
                if t.number is None or t.number < LAST:
                    take_x(m, k + 1)

            take_x(0, 0)
            over_tiles(dve, step)
            activate(0, LAST)

        @block.scalar
        def _(act):
            act.wait_ge(sem("shifted"), 1)
            act.activation(prob[:], work[:], ACT.Exp).then_inc(sem("exp_done"), 1)
            act.wait_ge(sem("weights_ready"), 1)

            def gate(m, k):
                t = Tile(m, k)
                act.wait_ge(sem("gu_filled"), t.i + 1)
                if not (t.number is not None and t.number < 2):
                    act.wait_ge(sem("act_lo"), t.i - 1)
                act.activation(gated[t.parity][:], bank_gu[:, t.parity, 0:F], ACT.Silu, scale=1.0 / X_SCALE).then_inc(sem("gated"), 1)
                act.wait_ge(sem("gu_taken"), t.i + 1)
                if not (t.number is not None and t.number < 2):
                    act.wait_ge(sem("a_filled"), t.i - 1)
                act.activation(act_hl[t.parity][:, 0], gated[t.parity][:], ACT.Copy).then_inc(sem("act_hi"), 1)

            def take_a(m, k):
                t = Tile(m, k)
                act.wait_ge(sem("a_filled"), t.i + 1)
                if not (t.number is not None and t.number < 2):
                    act.wait_ge(sem("y_filled"), t.i - 1)
                act.activation(aT[t.parity][:].rearrange("p h c t -> p (h c t)"),
                               bank_a[:, t.parity, 0:FC * P].bitcast(F16), ACT.Copy).then_inc(sem("a_taken"), 1)

            def take_y(m, k):
                t = Tile(m, k)
                act.wait_ge(sem("y_filled"), t.i + 1)
                if not (t.number is not None and t.number < 2):
                    act.wait_ge(sem("added"), 16 * (t.i - 1))
                act.activation(y[t.parity][:], bank_y[:, t.parity], ACT.Identity,
                               scale=t.column(slot_weight)).then_inc(sem("y_taken"), 1)

            def step(m, k):
                t = Tile(m, k)
                if t.number != 0:
                    gate(m, k - 1)
                    take_a(m, k - 1)
                    take_y(m, k - 1)

            over_tiles(act, step)
            for part in (gate, take_a, take_y):
                part(0, LAST)

        @block.tensor
        def _(pe):
            pe.wait_ge(sem("mask_ready"), 1)
            flat_mask = mask[:].rearrange("p t e -> p (t e)")
            pe.matmul(bank_r[:, 0, 0:NT * E], below[:], flat_mask, start=True, stop=True)
            pe.matmul(bank_r[:, 1, 0:NT * E], onesb[:], flat_mask, start=True, stop=True).then_inc(sem("ranked"), 1)
            pe.wait_ge(sem("packed"), 1)
            for n in range(K * NT):
                ins = pe.matmul(bank_y[:, 0, 0:3 * TILES], in_lane[:, n], packed[:, n].rearrange("p k t -> p (k t)"),
                                start=(n == 0), stop=(n == K * NT - 1))
            ins.then_inc(sem("sorted"), 1)
            pe.wait_ge(sem("experts_known"), 2)
            pe.wait_ge(sem("weights_ready"), 1)

            def transpose_x(m, k):
                t = Tile(m, k)
                pe.wait_ge(sem(f"gathered{t.parity}"), 16 * (t.half + 1))
                if not (t.number is not None and t.number < 2):
                    pe.wait_ge(sem("x_taken"), t.i - 1)
                bank = bank_x[:, t.parity].bitcast(F16)
                for n in range(2 * C):
                    ins = pe.transpose(bank[:, n * P:(n + 1) * P], xg[t.parity][:, n * P:(n + 1) * P], identh[:])
                ins.then_inc(sem("x_filled"), 1)

            def gate_up(m, k, offset, chunks):
                t = Tile(m, k)
                if chunks[0] == 0:
                    pe.wait_ge(sem("x_taken"), t.i + 1)
                    if not (t.number is not None and t.number < 2):
                        pe.wait_ge(sem("gu_taken"), t.i - 1)
                for c in chunks:
                    cols = bass.ds(offset + c * 2 * F, 2 * F)
                    for n, (lhs, rhs) in enumerate(((0, gu_hi_at), (0, gu_lo_at), (1, gu_hi_at))):
                        ins = pe.matmul(bank_gu[:, t.parity], xT[t.parity][:, lhs, c], rhs[:, cols],
                                        start=(c == 0 and n == 0), stop=(c == C - 1 and n == 2))
                if chunks[-1] == C - 1:
                    ins.then_inc(sem("gu_filled"), 1)

            def transpose_a(m, k):
                t = Tile(m, k)
                pe.wait_ge(sem("act_lo"), t.i + 1)
                if not (t.number is not None and t.number < 2):
                    pe.wait_ge(sem("a_taken"), t.i - 1)
                bank = bank_a[:, t.parity].bitcast(F16)
                for n in range(2 * FC):
                    ins = pe.transpose(bank[:, n * P:(n + 1) * P], act_hl[t.parity][:, n // FC, n % FC * P:(n % FC + 1) * P], identh[:])
                ins.then_inc(sem("a_filled"), 1)

            def down(m, k):
                t = Tile(m, k)
                pe.wait_ge(sem("a_taken"), t.i + 1)
                if not (t.number is not None and t.number < 2):
                    pe.wait_ge(sem("y_taken"), t.i - 1)
                offset = pe.value_load(t.column(dn_at)[0:1], min_val=0, max_val=(E - 1) * FC * D)
                for c in range(FC):
                    cols = bass.ds(offset + c * D, D)
                    for n, (lhs, rhs) in enumerate(((0, dn_hi_at), (0, dn_lo_at), (1, dn_hi_at))):
                        ins = pe.matmul(bank_y[:, t.parity], aT[t.parity][:, lhs, c], rhs[:, cols],
                                        start=(c == 0 and n == 0), stop=(c == FC - 1 and n == 2))
                ins.then_inc(sem("y_filled"), 1)

            def step(m, k):
                t = Tile(m, k)
                offset = pe.value_load(t.column(gu_at)[0:1], min_val=0, max_val=(E - 1) * C * 2 * F)
                if t.number is None or t.number < LAST:
                    transpose_x(m, k + 1)
                gate_up(m, k, offset, range(0, C // 2))
                if t.number != 0:
                    transpose_a(m, k - 1)
                gate_up(m, k, offset, range(C // 2, C))
                if t.number != 0:
                    down(m, k - 1)

            transpose_x(0, 0)
            over_tiles(pe, step)
            transpose_a(0, LAST)
            down(0, LAST)


_INS = ["x", "fside_BxS2xS2_0", "ctx_1024", "L0_ffn_router_w", "L0_ffn_gate_proj", "L0_ffn_up_proj", "L0_ffn_down_proj"]


def kernel(**inputs):
    import numpy as np
    import concourse.bacc as bacc
    from concourse.bass_utils import run_bass_kernel_spmd

    nc = bacc.Bacc("TRN2", target_bir_lowering=False, num_devices=1)
    arrays, args = {}, []
    for name in _INS:
        a = np.ascontiguousarray(inputs[name])
        arrays[f"in_{name}"] = a
        args.append(nc.dram_tensor(f"in_{name}", a.shape, mybir.dt.from_np(a.dtype), kind="ExternalInput").ap())
    B, T, D = arrays["in_x"].shape
    args.append(nc.dram_tensor("out", (B * T + P, D), F32, kind="ExternalOutput").ap())
    block_kernel(nc, *args)
    result = run_bass_kernel_spmd(nc, [arrays], core_ids=[0]).results[0]["out"]
    return result[:B * T].reshape(B, T, D)
```

```python
from contextlib import ExitStack
from functools import partial

import concourse.bass as bass
from concourse import mybir

F32 = mybir.dt.float32
F16 = mybir.dt.float16
BF16 = mybir.dt.bfloat16
I32 = mybir.dt.int32
ALU = mybir.AluOpType
ACT = mybir.ActivationFunctionType
AX = mybir.AxisListType

P = 128
LN_EPS = 1e-5
EPS = 1e-6
QMAX = 127.0
ROUND = 12582912.0
X_SCALE = 256.0
A_SCALE = 16.0
C_SCALE = 1024.0


SP_ORDER = ["load expert 0", "load x", "load expert 1", "load x again", "load expert 2", "load w1", "load w2",
            "load expert 3", "load expert 4", "load expert 5", "store x1", "store halves"]
POOL_ORDER = ["root 2", "smooth w2", "low 0", "low 1", "deviation 1", "residual", "root 1", "deviation 2", "smooth w1",
              "low 2", "low 3", "low 4", "low half", "low 5"]
DVE_ORDER = ["smoothing 2", "smooth a", "a scales", "w2 scales", "moments 1", "shift 1", "product 2", "w1 columns",
             "x columns", "ratio 1", "moments 2", "smoothing 1", "w2 columns", "shift 2", "smooth x", "x scales",
             "w1 scales", "product 1", "gate times up", "a columns", "ratio 2"]
ACT_ORDER = ["rows 2", "high 0", "high 1", "a up", "w2 up", "a transposed", "w2 scale row", "w2 transposed", "normalise 1",
             "high 2", "high 3", "high 4", "rows 1", "normalise 2", "tokens A", "x up", "w1 up", "scores A", "x transposed",
             "w1 transposed", "w1 scale row", "high half", "high 5", "silu", "tokens B", "scores B"]
PE_ORDER = ["rows 2", "a transposed", "w2 scale row", "w2 transposed", "product 2", "w1 columns", "x columns",
            "w2 columns", "rows 1", "tokens A", "scores A", "x transposed", "w1 transposed", "w1 scale row", "product 1",
            "tokens B", "a columns", "scores B"]
FIRST_HALF = {
    "load x", "load w1", "load w2", "moments 1", "deviation 1", "shift 1", "normalise 1", "w1 columns", "x columns",
    "ratio 1", "root 1", "smoothing 1", "rows 1", "smooth x", "x scales", "smooth w1", "w1 scales", "x up", "w1 up",
    "x transposed", "w1 transposed", "w1 scale row", "product 1", "silu", "gate times up", "w2 columns", "a columns",
    "ratio 2"}


def half_of(stage):
    return 0 if stage in FIRST_HALF else 1



class Signals:

    def __init__(self, nc, ctx):
        self.nc, self.ctx, self.made = nc, ctx, {}

    def __call__(self, name):
        if name not in self.made:
            self.made[name] = self.ctx.enter_context(self.nc.semaphore(name))
        return self.made[name]


class Ring:

    def __init__(self, psum, filled, taken, batches, order, taker_orders, uses):
        self.psum, self.filled, self.taken, self.batches, self.uses = psum, filled, taken, batches, uses
        self.order = [name for name in order if name in uses]
        assert sum(uses.values()) % 2 == 0
        for other in taker_orders:
            assert [name for name in other if name in uses] == self.order

    def sum_of(self, names):
        return sum(self.uses[name] for name in names)

    def before(self, stage, u, b):
        firsts, seconds = ([name for name in self.order if half_of(name) == half] for half in (0, 1))
        half = half_of(stage)
        if half == 0 and is_first(b):
            n, passes = self.sum_of(firsts[:firsts.index(stage)]) + u, 0
        elif half == 1 and isinstance(b, int) and b == self.batches - 1:
            n, passes = self.sum_of(firsts) + self.sum_of(seconds[:seconds.index(stage)]) + u, b
        else:
            n = self.sum_of(firsts) + self.sum_of(self.order[:self.order.index(stage)]) + u
            passes = b - 1 + half
        return passes * self.sum_of(self.order) + n, n % 2

    def fill(self, pe, stage, u, b):
        n, bank = self.before(stage, u, b)
        if not (isinstance(n, int) and n < 2):
            pe.wait_ge(self.taken, n - 1)
        return self.psum[:, bank]

    def empty(self, eng, stage, u, b):
        n, bank = self.before(stage, u, b)
        eng.wait_ge(self.filled, n + 1)
        return self.psum[:, bank]

    def emptied(self, eng, stage, u, b):
        eng.wait_ge(self.taken, self.before(stage, u, b)[0] + 1)


def upto(b, per_batch, j=None):
    return b * per_batch + (per_batch if j is None else j + 1)


def is_first(b):
    return isinstance(b, int) and b == 0


def block_kernel(nc, x, w1, w2, router_w, gate_w, up_w, down_w, out):
    B, T, D = x.shape
    O1 = w1.shape[1]
    I = w2.shape[2]
    E, _, F = gate_w.shape
    J = T // P
    C = D // P
    IC = I // P
    FC = F // P
    NT = B * J
    N = B * T
    TOPK = 2
    TILES = (N * TOPK + E * (P - 1)) // P
    EPB = E // B
    PPB = 3 * EPB
    assert [s for s in ACT_ORDER if s[:6] in ("tokens", "scores")] == ["tokens A", "scores A", "tokens B", "scores B"]
    assert TILES % 2 == 1 and O1 == T == D and 2 * I == O1 and C * F == FC * D

    halves_dram = nc.dram_tensor("token_halves", (N + P, 2 * D), F16).ap()

    with ExitStack() as ctx:
        def sb(name, shape, dt):
            return ctx.enter_context(nc.sbuf_tensor(name, shape, dt))

        def ps(name):
            return ctx.enter_context(nc.psum_tensor(name, [P, 2, 512], F32))

        sem = Signals(nc, ctx)

        gu_hi = sb("gu_hi", [P, E, C, 2 * F], F16)
        gu_lo = sb("gu_lo", [P, E, C, 2 * F], BF16)
        dn_hi = sb("dn_hi", [P, E, FC, D], F16)
        dn_lo = sb("dn_lo", [P, E, FC, D], BF16)
        identf = sb("identf", [P, P], F32)
        identh = sb("identh", [P, P], F16)
        below = sb("below", [P, P], BF16)
        onesb = sb("onesb", [P, P], BF16)
        power = sb("power", [P, 2, C], F32)
        rw = sb("rw", [P, C, E], F32)
        scores = sb("scores", [P, NT, E], F32)
        gather_at = sb("gather_at", [P, TILES], I32)
        slot_weight = sb("slot_weight", [P, TILES], F32)
        gu_at = sb("gu_at", [P, TILES], I32)
        dn_at = sb("dn_at", [P, TILES], I32)

        bank_t, bank_r, bank_q, bank_h = ps("bank_t"), ps("bank_r"), ps("bank_q"), ps("bank_h")

        hold_p = sb("hold_p", [P, 1], F32)
        hold_v = sb("hold_v", [P, 1], F32)

        def hold(pool):
            pool.tensor_tensor(hold_p[:], identf[:, 0:1], identf[:, 0:1], ALU.add)

        def spread(ap, shape, axis):
            return ap.unsqueeze(axis).to_broadcast(shape)

        def at(t, b):
            return t[:, b] if isinstance(b, int) else t[:, bass.ds(b, 1)].squeeze(1)

        def row_of(t, b):
            return t[b] if isinstance(b, int) else t[bass.ds(b, 1)].squeeze(0)


        zeros = sb("zeros", [P, D], F32)

        part1 = ExitStack()

        def tmp(name, shape, dt):
            return part1.enter_context(nc.sbuf_tensor(name, shape, dt))

        x_in = tmp("x_in", [P, J, D], F32)
        w1_in = tmp("w1_in", [P, J, D], F32)
        w2_in = tmp("w2_in", [P, J, I], F32)
        xn = tmp("xn", [P, J, D], F32)
        rows1 = tmp("rows1", [P, 3, D], F32)
        h = tmp("h", [P, J, O1], F32)
        xqT = tmp("xqT", [P, C, T], BF16)
        wqT = tmp("wqT", [P, C, O1], BF16)
        av = tmp("av", [P, J, I], F32)
        rows2 = tmp("rows2", [P, 2, I], F32)
        row_w2 = tmp("row_w2", [P, D], F32)
        aqT = tmp("aqT", [P, IC, T], BF16)
        dqT = tmp("dqT", [P, IC, D], BF16)
        x1 = tmp("x1", [P, J, D], F32)
        xn2 = tmp("xn2", [P, J, D], F32)
        halves = tmp("halves", [P, J, 2, D], F16)
        xn2T = tmp("xn2T", [P, 2, D], F32)
        stage = tmp("stage", [P, 3, C * F], F32)
        stats = tmp("stats", [P, 2, J, 6], F32)
        mv = tmp("mv", [P, 2, J, 2], F32)
        rstd = tmp("rstd", [P, 2, J], F32)
        shift = tmp("shift", [P, 2, J], F32)
        amax = [tmp(f"amax{k}", [P, 2, n], F32) for k, n in ((0, C), (1, IC))]
        ratio = [tmp(f"ratio{k}", [P, n], F32) for k, n in ((0, C), (1, IC))]
        smooth = [tmp(f"smooth{k}", [P, 2, n], F32) for k, n in ((0, C), (1, IC))]
        rmax = tmp("rmax", [P, 2, 2, J], F32)
        scale = tmp("scale", [P, 2, 2, J], F32)
        inv = tmp("inv", [P, 2, 2, J], F32)

        x_dram = x.rearrange("b (p j) d -> b p j d", j=J)
        out_dram = out[0:N].rearrange("(b p j) d -> b p j d", b=B, j=J)
        halves_out = halves_dram[0:N].rearrange("(b p j) d -> b p (j d)", b=B, j=J)
        w1_dram = w1.rearrange("b (j p) d -> b p j d", p=P)
        w2_dram = w2.rearrange("b (j p) i -> b p j i", p=P)
        expert_dram = (gate_w.rearrange("e (c p) f -> e p c f", p=P), up_w.rearrange("e (c p) f -> e p c f", p=P),
                       down_w.rearrange("e (c p) d -> e p c d", p=P))

        def staged(m):
            return stage[:, m % 3].rearrange("p (c f) -> p c f", c=C if m % 3 < 2 else FC)

        def parts(b, m):
            e = b * EPB + m // 3
            if m % 3 < 2:
                cols = slice(m % 3 * F, (m % 3 + 1) * F)
                return at(gu_hi, e)[:, :, cols], at(gu_lo, e)[:, :, cols]
            return at(dn_hi, e), at(dn_lo, e)

        ring_t = Ring(bank_t, sem("t_filled"), sem("t_taken"), B, PE_ORDER, (DVE_ORDER,),
                      {"w1 columns": C, "x columns": C, "w2 columns": IC, "a columns": IC})
        ring_r = Ring(bank_r, sem("r_filled"), sem("r_taken"), B, PE_ORDER, (ACT_ORDER,),
                      {"rows 1": 2, "w1 scale row": 1, "rows 2": 2, "w2 scale row": 1})
        ring_q = Ring(bank_q, sem("q_filled"), sem("q_taken"), B, PE_ORDER, (ACT_ORDER,),
                      {"x transposed": C, "w1 transposed": C, "a transposed": IC, "w2 transposed": IC,
                       "tokens A": 2, "tokens B": 2, "scores A": 1, "scores B": 1})
        ring_h = Ring(bank_h, sem("h_filled"), sem("h_taken"), B, PE_ORDER, (DVE_ORDER,), {"product 1": J, "product 2": J})

        def woven(eng, order, steps):
            assert set(order) == set(steps)

            def run(names, b):
                for name in names:
                    steps[name](b + 1 - half_of(name))

            run([name for name in order if half_of(name) == 0], -1)
            run(order, 0)
            with eng.Fori(1, B - 1) as b:
                run(order, b)
            run([name for name in order if half_of(name) == 1], B - 1)

        block = part1.enter_context(nc.Block())

        @block.sync
        def _(sp):
            sp.dma_start(rw[:], router_w.rearrange("(c p) e -> p c e", p=P)).then_inc(sem("router_in"), 16)

            def load_x(b):
                if not is_first(b):
                    sp.wait_ge(sem("xn_ready"), upto(b, J) - J)
                sp.dma_start(x_in[:], row_of(x_dram, b)).then_inc(sem("x_in"), 16)

            def load_w1(b):
                if not is_first(b):
                    sp.wait_ge(ring_q.filled, ring_q.before("w1 transposed", C - 1, b - 1)[0] + 1)
                sp.dma_start(w1_in[:], row_of(w1_dram, b)).then_inc(sem("w1_in"), 16)

            def load_w2(b):
                if not is_first(b):
                    sp.wait_ge(ring_q.filled, ring_q.before("w2 transposed", IC - 1, b - 1)[0] + 1)
                sp.dma_start(w2_in[:], row_of(w2_dram, b)).then_inc(sem("w2_in"), 16)

            def load_x_again(b):
                if not is_first(b):
                    stored = 16 * (upto(b, 1) - 1)
                    sp.wait_ge(sem("x1_stored"), stored)
                    sp.wait_ge(sem("halves_stored"), stored)
                sp.dma_start(x1[:], row_of(x_dram, b)).then_inc(sem("x_again"), 16)

            def load_expert(m, b):
                if not (is_first(b) and m < 3):
                    sp.wait_ge(sem("lo_done"), upto(b, PPB, m) - 3)
                sp.dma_start(staged(m), row_of(expert_dram[m % 3], b * EPB + m // 3)).then_inc(sem(f"stage_in{m % 3}"), 16)

            def store_x1(b):
                sp.wait_ge(sem("x1_ready"), upto(b, J))
                sp.dma_start(row_of(out_dram, b), x1[:]).then_inc(sem("x1_stored"), 16)

            def store_halves(b):
                sp.wait_ge(sem("hi_half"), upto(b, 1))
                sp.wait_ge(sem("lo_half"), upto(b, 1))
                sp.dma_start(row_of(halves_out, b), halves[:].rearrange("p j k d -> p (j k d)")).then_inc(sem("halves_stored"), 16)

            woven(sp, SP_ORDER,
                  {"load x": load_x, "load w1": load_w1, "load w2": load_w2, "load x again": load_x_again,
                   "store x1": store_x1, "store halves": store_halves,
                   **{f"load expert {m}": partial(load_expert, m) for m in range(PPB)}})
            sp.wait_ge(sem("zeroed"), 1)
            sp.dma_start(out[N:N + P], zeros[:]).then_inc(sem("pad_stored"), 16)
            sp.dma_start(halves_dram[N:N + P], zeros[:].bitcast(F16)).then_inc(sem("pad_stored"), 16)
            sp.wait_ge(sem("pad_stored"), 32)
            sp.wait_ge(sem("router_in"), 16)
            sp.wait_ge(sem("x1_stored"), 16 * B)
            sp.wait_ge(sem("halves_stored"), 16 * B)

        @block.gpsimd
        def _(pool):
            pool.memset(identf[:], 0.0).then_inc(sem("blank"), 1)
            pool.memset(below[:], 1.0).then_inc(sem("blank"), 1)
            pool.memset(power[:, 0], -0.5).then_inc(sem("constants"), 1)
            pool.memset(power[:, 1], 0.5).then_inc(sem("constants"), 1)
            pool.wait_ge(sem("blank"), 2)
            pool.affine_select(out=identf[:], in_=identf[:], compare_op=ALU.not_equal, fill=1.0, base=0,
                               pattern=[[-1, P]], channel_multiplier=1).then_inc(sem("constants"), 1)
            pool.affine_select(out=below[:], in_=below[:], compare_op=ALU.is_gt, fill=0.0, base=0,
                               pattern=[[1, P]], channel_multiplier=-1).then_inc(sem("constants"), 1)
            pool.wait_ge(sem("constants"), 4)
            pool.tensor_copy(identh[:], identf[:]).then_inc(sem("idents"), 1)
            pool.memset(onesb[:], 1.0).then_inc(sem("constants"), 1)
            pool.memset(zeros[:], 0.0).then_inc(sem("zeroed"), 1)

            def low(m, b):
                hi, lo = parts(b, m)
                pool.wait_ge(sem("hi_done"), upto(b, PPB, m))
                pool.tensor_tensor(lo, staged(m), hi, ALU.subtract).then_inc(sem("lo_done"), 1)

            def root(out_ap, in_ap, which, ready, done, b):
                pool.wait_ge(ready, upto(b, 1))
                pool.tensor_tensor(out_ap, in_ap, power[:, which, 0:in_ap.shape[1]], ALU.pow).then_inc(done, 1)

            def deviation(which, b):
                root(rstd[:, which], mv[:, which, :, 1], 0, sem(f"var{which}"), sem(f"rstd{which}"), b)

            def smoothing_root(which, b):
                root(smooth[which][:, 1], ratio[which][:], 1, sem(f"ratio{which}"), sem(f"root{which}"), b)

            def smooth_w1(b):
                ring_r.emptied(pool, "rows 1", 1, b)
                for j in range(0, J, J // 2):
                    rows = w1_in[:, j:j + J // 2]
                    pool.tensor_tensor(rows, rows, spread(rows1[:, 1], [P, J // 2, D], 1), ALU.mult).then_inc(sem("ws_ready"), 1)

            def smooth_w2(b):
                ring_r.emptied(pool, "rows 2", 1, b)
                pool.tensor_tensor(w2_in[:], w2_in[:], spread(rows2[:, 1], [P, J, I], 1), ALU.mult).then_inc(sem("ds_ready"), 1)

            def residual(b):
                pool.wait_ge(sem("x_again"), 16 * upto(b, 1))
                for j in range(J):
                    ring_h.emptied(pool, "product 2", j, b)
                    pool.tensor_tensor(x1[:, j], x1[:, j], xn2[:, j], ALU.add).then_inc(sem("x1_ready"), 1)

            def low_half(b):
                pool.wait_ge(sem("xn2_ready"), upto(b, J))
                pool.wait_ge(sem("hi_half"), upto(b, 1))
                if not is_first(b):
                    pool.wait_ge(sem("halves_stored"), 16 * (upto(b, 1) - 1))
                pool.tensor_tensor(halves[:, :, 1], xn2[:], halves[:, :, 0], ALU.subtract).then_inc(sem("lo_half"), 1)

            woven(pool, POOL_ORDER,
                  {"deviation 1": partial(deviation, 0), "root 1": partial(smoothing_root, 0), "smooth w1": smooth_w1,
                   "root 2": partial(smoothing_root, 1), "smooth w2": smooth_w2, "residual": residual,
                   "deviation 2": partial(deviation, 1), "low half": low_half,
                   **{f"low {m}": partial(low, m) for m in range(PPB)}})

        @block.vector
        def _(dve):
            def moments(b, which, src, ready, per_batch):
                for j in range(J):
                    if j < per_batch:
                        dve.wait_ge(ready, upto(b, per_batch, j) * (16 if per_batch == 1 else 1))
                    dve.bn_stats(stats[:, which, j], src[:, j]).then_inc(sem(f"stats{which}"), 1)
                dve.wait_ge(sem(f"stats{which}"), upto(b, J))
                dve.tensor_copy(hold_v[:], stats[:, which, 0, 0:1])
                for j in range(J):
                    dve.bn_aggr(mv[:, which, j], stats[:, which, j]).then_inc(sem(f"moments{which}"), 1)
                dve.wait_ge(sem(f"moments{which}"), upto(b, J))
                dve.tensor_scalar(mv[:, which, :, 1], mv[:, which, :, 1], LN_EPS, None, ALU.add).then_inc(sem(f"var{which}"), 1)

            def shift_of(which):
                dve.scalar_tensor_tensor(out=shift[:, which], in0=mv[:, which, :, 0], scalar=-1.0, in1=rstd[:, which],
                                         op0=ALU.mult, op1=ALU.mult).then_inc(sem(f"shift{which}"), 1)

            def shift1(b):
                dve.wait_ge(sem("rstd0"), upto(b, 1))
                shift_of(0)

            def shift2(b):
                dve.wait_ge(sem("rstd1"), upto(b, 1))
                dve.tensor_scalar(rstd[:, 1], rstd[:, 1], X_SCALE, None, ALU.mult).then_inc(sem("rstd1_scaled"), 1)
                dve.wait_ge(sem("rstd1_scaled"), upto(b, 1))
                shift_of(1)

            def column_max(stage, dst, chunks, b):
                for c in range(chunks):
                    bank = ring_t.empty(dve, stage, c, b)
                    dve.tensor_reduce(dst[:, c:c + 1], bank, AX.X, ALU.max,
                                      apply_absolute_value=True).then_inc(ring_t.taken, 1)

            def smoothing_ratio(which, last_stages, b):
                done = sem(f"clamped{which}")
                for stage in last_stages:
                    ring_t.emptied(dve, stage, amax[which].shape[2] - 1, b)
                dve.tensor_scalar(amax[which][:], amax[which][:], EPS, None, ALU.max).then_inc(done, 1)
                dve.wait_ge(done, upto(b, 2, 0))
                dve.reciprocal(ratio[which][:], amax[which][:, 1]).then_inc(done, 1)
                dve.wait_ge(done, upto(b, 2, 1))
                dve.tensor_tensor(ratio[which][:], ratio[which][:], amax[which][:, 0], ALU.mult).then_inc(sem(f"ratio{which}"), 1)

            def smoothing(which, b):
                done = sem(f"smooth{which}")
                dve.wait_ge(sem(f"root{which}"), upto(b, 1))
                dve.tensor_scalar(smooth[which][:, 1], smooth[which][:, 1], EPS, None, ALU.max).then_inc(done, 1)
                dve.wait_ge(done, upto(b, 2, 0))
                dve.reciprocal(smooth[which][:, 0], smooth[which][:, 1]).then_inc(done, 1)

            def row_scales(which, side, src, ready, cuts, b):
                done = sem(f"row_max{which}{side}")
                for n in range(cuts):
                    rows = slice(n * J // cuts, (n + 1) * J // cuts)
                    dve.wait_ge(ready, upto(b, cuts, n))
                    dve.tensor_reduce(rmax[:, which, side, rows], src[:, rows], AX.X, ALU.max, apply_absolute_value=True).then_inc(done, 1)
                    dve.wait_ge(done, upto(b, 2 * cuts, 2 * n))
                    dve.tensor_scalar(scale[:, which, side, rows], rmax[:, which, side, rows], EPS, 1.0 / QMAX, ALU.max,
                                      ALU.mult).then_inc(done, 1)
                    dve.wait_ge(done, upto(b, 2 * cuts, 2 * n + 1))
                    dve.reciprocal(inv[:, which, side, rows], scale[:, which, side, rows]).then_inc(sem(f"inv{which}{side}"), 1)

            def smooth_x(b):
                ring_r.emptied(dve, "rows 1", 0, b)
                for j in range(0, J, J // 2):
                    rows = xn[:, j:j + J // 2]
                    dve.tensor_tensor(rows, rows, spread(rows1[:, 0], [P, J // 2, D], 1), ALU.mult).then_inc(sem("xs_ready"), 1)

            def smooth_a(b):
                ring_r.emptied(dve, "rows 2", 0, b)
                dve.tensor_tensor(av[:], av[:], spread(rows2[:, 0], [P, J, I], 1), ALU.mult).then_inc(sem("as_ready"), 1)

            def product1(b):
                ring_r.emptied(dve, "w1 scale row", 0, b)
                if not is_first(b):
                    dve.wait_ge(sem("silu_done"), upto(b, 1) - 1)
                for j in range(J):
                    bank = ring_h.empty(dve, "product 1", j, b)
                    dve.scalar_tensor_tensor(out=h[:, j], in0=bank, scalar=scale[:, 0, 0, j:j + 1], in1=rows1[:, 2],
                                             op0=ALU.mult, op1=ALU.mult).then_inc(ring_h.taken, 1)

            def gate_times_up(b):
                dve.wait_ge(sem("silu_done"), upto(b, 1))
                dve.tensor_tensor(av[:], av[:], h[:, :, I:2 * I], ALU.mult).then_inc(sem("a_ready"), 1)

            def product2(b):
                ring_r.emptied(dve, "w2 scale row", 0, b)
                if not is_first(b):
                    dve.wait_ge(sem("lo_half"), upto(b, 1) - 1)
                    ring_q.emptied(dve, "tokens B", 1, b - 1)
                for j in range(J):
                    bank = ring_h.empty(dve, "product 2", j, b)
                    dve.scalar_tensor_tensor(out=xn2[:, j], in0=bank, scalar=scale[:, 1, 0, j:j + 1], in1=row_w2[:],
                                             op0=ALU.mult, op1=ALU.mult).then_inc(ring_h.taken, 1)

            woven(dve, DVE_ORDER,
                  {"moments 1": lambda b: moments(b, 0, x_in, sem("x_in"), 1), "shift 1": shift1,
                   "w1 columns": partial(column_max, "w1 columns", amax[0][:, 1], C),
                   "x columns": partial(column_max, "x columns", amax[0][:, 0], C),
                   "ratio 1": partial(smoothing_ratio, 0, ("w1 columns", "x columns")),
                   "smoothing 1": partial(smoothing, 0), "smooth x": smooth_x,
                   "x scales": partial(row_scales, 0, 0, xn[:], sem("xs_ready"), 2),
                   "w1 scales": partial(row_scales, 0, 1, w1_in[:], sem("ws_ready"), 2),
                   "product 1": product1, "gate times up": gate_times_up,
                   "w2 columns": partial(column_max, "w2 columns", amax[1][:, 1], IC),
                   "a columns": partial(column_max, "a columns", amax[1][:, 0], IC),
                   "ratio 2": partial(smoothing_ratio, 1, ("w2 columns", "a columns")),
                   "smoothing 2": partial(smoothing, 1), "smooth a": smooth_a,
                   "a scales": partial(row_scales, 1, 0, av[:], sem("as_ready"), 1),
                   "w2 scales": partial(row_scales, 1, 1, w2_in[:], sem("ds_ready"), 1),
                   "product 2": product2, "moments 2": lambda b: moments(b, 1, x1, sem("x1_ready"), J), "shift 2": shift2})

        @block.scalar
        def _(act):
            def normalise(b, which, src, dst, done):
                act.wait_ge(sem(f"shift{which}"), upto(b, 1))
                for j in range(J):
                    act.activation(dst[:, j], src[:, j], ACT.Identity, bias=shift[:, which, j:j + 1],
                                   scale=rstd[:, which, j:j + 1]).then_inc(done, 1)

            def normalise1(b):
                if not is_first(b):
                    act.wait_ge(ring_q.filled, ring_q.before("x transposed", C - 1, b - 1)[0] + 1)
                normalise(b, 0, x_in, xn, sem("xn_ready"))

            def take_row(stage, u, b, dst):
                bank = ring_r.empty(act, stage, u, b)
                act.activation(dst, bank[:, 0:dst.shape[1]], ACT.Copy).then_inc(ring_r.taken, 1)

            def smoothing_rows(stage, users, dst, b):
                if not is_first(b):
                    for name, per_batch in users:
                        act.wait_ge(sem(name), upto(b, per_batch) - per_batch)
                take_row(stage, 0, b, dst[:, 0])
                take_row(stage, 1, b, dst[:, 1])

            def scale_row(stage, product, dst, b):
                if not is_first(b):
                    ring_h.emptied(act, product, J - 1, b - 1)
                take_row(stage, 0, b, dst)

            def scale_up(which, side, t, cuts, done, b):
                for j in range(J):
                    if j % (J // cuts) == 0:
                        act.wait_ge(sem(f"inv{which}{side}"), upto(b, cuts, j * cuts // J))
                    ins = act.activation(t[:, j], t[:, j], ACT.Identity, bias=ROUND, scale=inv[:, which, side, j:j + 1])
                ins.then_inc(done, 1)

            def take_transposed(stage, dst, chunks, product, b):
                if not is_first(b):
                    act.wait_ge(ring_h.filled, ring_h.before(product, J - 1, b - 1)[0] + 1)
                for c in range(chunks):
                    bank = ring_q.empty(act, stage, c, b)
                    act.activation(dst[:, c], bank, ACT.Identity, bias=-ROUND).then_inc(ring_q.taken, 1)

            def high(m, b):
                hi, _ = parts(b, m)
                act.wait_ge(sem(f"stage_in{m % 3}"), 16 * upto(b, EPB, m // 3))
                act.activation(hi, staged(m), ACT.Copy).then_inc(sem("hi_done"), 1)

            def silu(b):
                if not is_first(b):
                    act.wait_ge(ring_q.filled, ring_q.before("a transposed", IC - 1, b - 1)[0] + 1)
                ring_h.emptied(act, "product 1", J - 1, b)
                act.activation(av[:], h[:, :, 0:I], ACT.Silu).then_inc(sem("silu_done"), 1)

            def high_half(b):
                act.wait_ge(sem("xn2_ready"), upto(b, J))
                if not is_first(b):
                    act.wait_ge(sem("halves_stored"), 16 * (upto(b, 1) - 1))
                act.activation(halves[:, :, 0], xn2[:], ACT.Copy).then_inc(sem("hi_half"), 1)

            def take_tokens(stage, b):
                for j in range(2):
                    bank = ring_q.empty(act, stage, j, b)
                    act.activation(xn2T[:, j], bank, ACT.Copy).then_inc(ring_q.taken, 1)

            def take_scores(stage, pair, b):
                bank = ring_q.empty(act, stage, 0, b)
                tile = b * J + 2 * pair
                dst = scores[:, tile:tile + 2] if isinstance(b, int) else scores[:, bass.ds(tile, 2)]
                act.activation(dst, bank[:, 0:2 * E].rearrange("p (j e) -> p j e", e=E), ACT.Copy,
                               scale=1.0 / X_SCALE).then_inc(ring_q.taken, 1)

            woven(act, ACT_ORDER,
                  {"normalise 1": normalise1, "rows 1": partial(smoothing_rows, "rows 1", (("xs_ready", 2), ("ws_ready", 2)), rows1),
                   "x up": partial(scale_up, 0, 0, xn, 2, sem("xq_up")), "w1 up": partial(scale_up, 0, 1, w1_in, 2, sem("wq_up")),
                   "x transposed": partial(take_transposed, "x transposed", xqT, C, "product 1"),
                   "w1 transposed": partial(take_transposed, "w1 transposed", wqT, C, "product 1"),
                   "w1 scale row": partial(scale_row, "w1 scale row", "product 1", rows1[:, 2]), "silu": silu,
                   "rows 2": partial(smoothing_rows, "rows 2", (("as_ready", 1), ("ds_ready", 1)), rows2),
                   "a up": partial(scale_up, 1, 0, av, 1, sem("aq_up")), "w2 up": partial(scale_up, 1, 1, w2_in, 1, sem("dq_up")),
                   "a transposed": partial(take_transposed, "a transposed", aqT, IC, "product 2"),
                   "w2 transposed": partial(take_transposed, "w2 transposed", dqT, IC, "product 2"),
                   "w2 scale row": partial(scale_row, "w2 scale row", "product 2", row_w2[:]),
                   "normalise 2": lambda b: normalise(b, 1, x1, xn2, sem("xn2_ready")), "high half": high_half,
                   "tokens A": partial(take_tokens, "tokens A"), "tokens B": partial(take_tokens, "tokens B"),
                   "scores A": partial(take_scores, "scores A", 0), "scores B": partial(take_scores, "scores B", 1),
                   **{f"high {m}": partial(high, m) for m in range(PPB)}})

        @block.tensor
        def _(pe):
            pe.wait_ge(sem("constants"), 4)
            pe.wait_ge(sem("idents"), 1)
            pe.wait_ge(sem("router_in"), 16)

            def transposed(ring, stage, src, chunks, ready, per_batch, b):
                pe.wait_ge(ready, upto(b, per_batch))
                for c in range(chunks):
                    bank = ring.fill(pe, stage, c, b)
                    for j in range(J):
                        ins = pe.transpose(bank[:, j * P:(j + 1) * P], src[:, j, c * P:(c + 1) * P], identf[:])
                    ins.then_inc(ring.filled, 1)

            def as_row(stage, u, b, columns):
                bank = ring_r.fill(pe, stage, u, b)
                n = columns.shape[1]
                for c in range(n):
                    ins = pe.matmul(bank[:, c * P:(c + 1) * P], columns[:, c:c + 1].to_broadcast([P, P]), identf[:],
                                    start=True, stop=True)
                ins.then_inc(ring_r.filled, 1)

            def smoothing_rows(stage, which, b):
                pe.wait_ge(sem(f"smooth{which}"), upto(b, 2))
                as_row(stage, 0, b, smooth[which][:, 0])
                as_row(stage, 1, b, smooth[which][:, 1])

            def scale_row(stage, which, cuts, b):
                pe.wait_ge(sem(f"inv{which}1"), upto(b, cuts))
                as_row(stage, 0, b, scale[:, which, 1])

            def product(stage, lhs, rhs, sources, b):
                for source in sources:
                    ring_q.emptied(pe, source, lhs.shape[1] - 1, b)
                for j in range(J):
                    bank = ring_h.fill(pe, stage, j, b)
                    for c in range(lhs.shape[1]):
                        ins = pe.matmul(bank, lhs[:, c, j * P:(j + 1) * P], rhs[:, c], start=(c == 0), stop=(c == lhs.shape[1] - 1))
                    ins.then_inc(ring_h.filled, 1)

            def tokens(stage, pair, b):
                pe.wait_ge(sem("xn2_ready"), upto(b, J, 2 * pair + 1))
                for j in range(2):
                    bank = ring_q.fill(pe, stage, j, b)
                    for c in range(C):
                        ins = pe.transpose(bank[:, c * P:(c + 1) * P], xn2[:, 2 * pair + j, c * P:(c + 1) * P], identf[:])
                    ins.then_inc(ring_q.filled, 1)

            def router(stage, source, b):
                ring_q.emptied(pe, source, 1, b)
                bank = ring_q.fill(pe, stage, 0, b)
                for j in range(2):
                    for c in range(C):
                        ins = pe.matmul(bank[:, j * E:(j + 1) * E], xn2T[:, j, c * P:(c + 1) * P], rw[:, c],
                                        start=(c == 0), stop=(c == C - 1))
                ins.then_inc(ring_q.filled, 1)

            def columns(stage, src, chunks, ready, per_batch):
                return partial(transposed, ring_t, stage, src, chunks, ready, per_batch)

            def quantised(stage, src, chunks, ready):
                return partial(transposed, ring_q, stage, src, chunks, ready, 1)

            def loaded(stage, src, chunks, ready):
                def run(b):
                    pe.wait_ge(ready, 16 * upto(b, 1))
                    for c in range(chunks):
                        bank = ring_t.fill(pe, stage, c, b)
                        for j in range(J):
                            ins = pe.transpose(bank[:, j * P:(j + 1) * P], src[:, j, c * P:(c + 1) * P], identf[:])
                        ins.then_inc(ring_t.filled, 1)
                return run

            woven(pe, PE_ORDER,
                  {"w1 columns": loaded("w1 columns", w1_in, C, sem("w1_in")),
                   "x columns": columns("x columns", xn, C, sem("xn_ready"), J),
                   "rows 1": partial(smoothing_rows, "rows 1", 0),
                   "x transposed": quantised("x transposed", xn, C, sem("xq_up")),
                   "w1 transposed": quantised("w1 transposed", w1_in, C, sem("wq_up")),
                   "w1 scale row": partial(scale_row, "w1 scale row", 0, 2),
                   "product 1": partial(product, "product 1", xqT, wqT, ("x transposed", "w1 transposed")),
                   "w2 columns": loaded("w2 columns", w2_in, IC, sem("w2_in")),
                   "a columns": columns("a columns", av, IC, sem("a_ready"), 1),
                   "rows 2": partial(smoothing_rows, "rows 2", 1),
                   "a transposed": quantised("a transposed", av, IC, sem("aq_up")),
                   "w2 transposed": quantised("w2 transposed", w2_in, IC, sem("dq_up")),
                   "w2 scale row": partial(scale_row, "w2 scale row", 1, 1),
                   "product 2": partial(product, "product 2", aqT, dqT, ("a transposed", "w2 transposed")),
                   "tokens A": partial(tokens, "tokens A", 0), "tokens B": partial(tokens, "tokens B", 1),
                   "scores A": partial(router, "scores A", "tokens A"), "scores B": partial(router, "scores B", "tokens B")})

        part1.close()

        K = TOPK

        def buf(name, shape, dt=F32):
            return ctx.enter_context(nc.sbuf_tensor(name, shape, dt))

        lane = buf("lane", [P, P])
        preference = buf("preference", [P, E])
        token = buf("token", [P, NT])
        pad_row = buf("pad_row", [P, 1])
        prob = buf("prob", [P, NT, E])
        work = buf("work", [P, NT, E])
        best = buf("best", [P, K, NT])
        pick = buf("pick", [P, K, NT])
        chosen = buf("chosen", [P, K, NT, E])
        mask = buf("mask", [P, NT, E], BF16)
        run_a = buf("run_a", [P, NT, E])
        run_b = buf("run_b", [P, NT, E])
        total = buf("total", [P, NT])
        ends = [buf(f"ends{i}", [P, E]) for i in range(2)]
        count = buf("count", [P, E])
        slot = buf("slot", [P, NT, E])
        pos = buf("pos", [P, K, NT])
        tile_of = buf("tile_of", [P, K, NT])
        lane_of = buf("lane_of", [P, K, NT])
        weight = buf("weight", [P, K, NT])
        weight_hi = buf("weight_hi", [P, K, NT], F16)
        weight_lo = buf("weight_lo", [P, K, NT])
        in_lane = buf("in_lane", [P, K * NT, P], F16)
        in_tile = buf("in_tile", [P, K * NT, TILES])
        packed = buf("packed", [P, K * NT, 3, TILES], F16)
        expert_of = buf("expert_of", [P, TILES])
        ended = buf("ended", [P, TILES, E])
        unused = buf("unused", [P, TILES])
        table = buf("table", [P, 3 * TILES])
        gather_idx = [buf(f"gather_idx{k}", [P, 1], I32) for k in range(2)]
        scatter_idx = [buf(f"scatter_idx{k}", [P, 1], I32) for k in range(2)]
        xg = [buf(f"xg{k}", [P, 2 * D], F16) for k in range(2)]
        xT = [buf(f"xT{k}", [P, 2, C, P], F16) for k in range(2)]
        gated = [buf(f"gated{k}", [P, F]) for k in range(2)]
        act_hl = [buf(f"act_hl{k}", [P, 2, F], F16) for k in range(2)]
        aT = [buf(f"aT{k}", [P, 2, FC, P], F16) for k in range(2)]
        y = [buf(f"y{k}", [P, D]) for k in range(2)]

        bank_x, bank_gu, bank_a, bank_y = bank_t, bank_r, bank_q, bank_h
        gu_hi_at, gu_lo_at = (t[:].rearrange("p e c f -> p (e c f)") for t in (gu_hi, gu_lo))
        dn_hi_at, dn_lo_at = (t[:].rearrange("p e c d -> p (e c d)") for t in (dn_hi, dn_lo))
        acc_rows = out
        LAST = TILES - 1

        class Tile:

            def __init__(self, m, k):
                self.parity, self.half, self.i = k % 2, m + k // 2, 2 * m + k
                self.number = self.i if isinstance(self.i, int) else None

            def column(self, t):
                return t[:, self.i:self.i + 1] if self.number is not None else t[:, bass.ds(self.i, 1)]

        def over_tiles(eng, step):
            for k in range(3):
                step(0, k)
            with eng.Fori(1, (TILES - 3) // 2) as m:
                step(m, 1)
                step(m, 2)
            step(0, TILES - 2)
            step(0, TILES - 1)

        block = ctx.enter_context(nc.Block())

        @block.gpsimd
        def _(pool):
            pool.iota(lane[:], [[1, P]], base=0, channel_multiplier=0, allow_small_or_imprecise_dtypes=True).then_inc(sem("numbers"), 1)
            pool.iota(preference[:], [[-1, E]], base=E, channel_multiplier=0, allow_small_or_imprecise_dtypes=True).then_inc(sem("numbers"), 1)
            pool.iota(token[:].rearrange("p (b j) -> p b j", b=B), [[T, B], [1, J]], base=1, channel_multiplier=J,
                      allow_small_or_imprecise_dtypes=True).then_inc(sem("numbers"), 1)
            pool.iota(pad_row[:], [[0, 1]], base=N + 1, channel_multiplier=1, allow_small_or_imprecise_dtypes=True).then_inc(sem("numbers"), 1)

            def gather(m, k):
                t = Tile(m, k)
                if not (t.number is not None and t.number < 2):
                    pool.wait_ge(sem("x_filled"), t.i - 1)
                pool.tensor_copy(gather_idx[t.parity][:], t.column(gather_at)).then_inc(sem("gather_idx"), 1)
                pool.wait_ge(sem("gather_idx"), t.i + 1)
                hold(pool)
                pool.indirect_dma_start(out=xg[t.parity][:], out_offset=None, in_=halves_dram,
                                        in_offset=bass.IndirectOffsetOnAxis(ap=gather_idx[t.parity][:, 0:1], axis=0)
                                        ).then_inc(sem(f"gathered{t.parity}"), 16)

            def scatter(m, k):
                t = Tile(m, k)
                pool.tensor_copy(scatter_idx[t.parity][:], t.column(gather_at)).then_inc(sem("scatter_idx"), 1)
                pool.wait_ge(sem("scatter_idx"), t.i + 1)
                pool.wait_ge(sem("y_taken"), t.i + 1)
                if t.number != 0:
                    pool.wait_ge(sem("added"), 16 * t.i)
                hold(pool)
                pool.indirect_dma_start(out=acc_rows, out_offset=bass.IndirectOffsetOnAxis(ap=scatter_idx[t.parity][:, 0:1], axis=0),
                                        in_=y[t.parity][:], in_offset=None, compute_op=ALU.add).then_inc(sem("added"), 16)

            pool.wait_ge(sem("gather_ready"), 1)
            for k in range(3):
                gather(0, k)
            def step(m, k):
                t = Tile(m, k)
                if t.number is None or t.number + 3 < TILES:
                    gather(m, k + 3)
                if t.number != 0:
                    scatter(m, k - 1)
            for k in range(3):
                step(0, k)
            with pool.Fori(1, (TILES - 5) // 2) as m:
                step(m, 1)
                step(m, 2)
            for k in range(TILES - 4, TILES):
                step(0, k)
            scatter(0, LAST)
            pool.wait_ge(sem("added"), 16 * TILES)

        @block.vector
        def _(dve):
            steps = [0]

            def then(ins):
                steps[0] += 1
                ins.then_inc(sem("route"), 1)
                dve.wait_ge(sem("route"), steps[0])

            shape = [P, NT, E]
            dve.wait_ge(sem("numbers"), 4)
            then(dve.tensor_reduce(total[:], scores[:], AX.X, ALU.max))
            dve.tensor_tensor(work[:], scores[:], spread(total[:], shape, 2), ALU.subtract).then_inc(sem("shifted"), 1)
            dve.wait_ge(sem("exp_done"), 1)
            then(dve.tensor_reduce(total[:], prob[:], AX.X, ALU.add))
            then(dve.reciprocal(total[:], total[:]))
            then(dve.tensor_tensor(prob[:], prob[:], spread(total[:], shape, 2), ALU.mult))
            for k in range(K):
                then(dve.tensor_reduce(best[:, k], prob[:], AX.X, ALU.max))
                then(dve.tensor_tensor(work[:], prob[:], spread(best[:, k], shape, 2), ALU.is_equal))
                then(dve.tensor_tensor(work[:], work[:], spread(preference[:], shape, 1), ALU.mult))
                then(dve.tensor_reduce(pick[:, k], work[:], AX.X, ALU.max))
                then(dve.tensor_tensor(chosen[:, k], spread(preference[:], shape, 1), spread(pick[:, k], shape, 2), ALU.is_equal))
                if k == 0:
                    then(dve.scalar_tensor_tensor(out=prob[:], in0=chosen[:, 0], scalar=-2.0, in1=prob[:], op0=ALU.mult, op1=ALU.add))
            dve.tensor_tensor(mask[:], chosen[:, 0], chosen[:, 1], ALU.add).then_inc(sem("mask_ready"), 1)
            then(dve.tensor_tensor(total[:], best[:, 0], best[:, 1], ALU.add))
            then(dve.reciprocal(total[:], total[:]))
            then(dve.tensor_scalar(total[:], total[:], C_SCALE, None, ALU.mult))
            then(dve.tensor_tensor(weight[:], best[:], spread(total[:], [P, K, NT], 1), ALU.mult))
            then(dve.tensor_copy(weight_hi[:], weight[:]))
            then(dve.tensor_tensor(weight_lo[:], weight[:], weight_hi[:], ALU.subtract))
            dve.wait_ge(sem("ranked"), 1)
            then(dve.tensor_copy(run_a[:].rearrange("p t e -> p (t e)"), bank_r[:, 1, 0:NT * E]))
            then(dve.tensor_copy(slot[:].rearrange("p t e -> p (t e)"), bank_r[:, 0, 0:NT * E]))
            then(dve.tensor_tensor(slot[:], slot[:], run_a[:], ALU.subtract))
            a, b2 = run_a, run_b
            step = 1
            while step < NT:
                dve.tensor_copy(b2[:, 0:step], a[:, 0:step])
                then(dve.tensor_tensor(b2[:, step:], a[:, step:], a[:, :NT - step], ALU.add))
                a, b2, step = b2, a, 2 * step
            then(dve.tensor_scalar(count[:], a[:, NT - 1], 1.0 / P, 0.5 - 0.5 / P, ALU.mult, ALU.add))
            then(dve.tensor_scalar(count[:], count[:], ROUND, ROUND, ALU.add, ALU.subtract))
            then(dve.tensor_copy(ends[0][:], count[:]))
            c, d, step = ends[0], ends[1], 1
            while step < E:
                dve.tensor_copy(d[:, 0:step], c[:, 0:step])
                then(dve.tensor_tensor(d[:, step:], c[:, step:], c[:, :E - step], ALU.add))
                c, d, step = d, c, 2 * step
            then(dve.tensor_tensor(count[:], c[:], count[:], ALU.subtract))
            then(dve.tensor_scalar(count[:], count[:], float(P), None, ALU.mult))
            then(dve.tensor_tensor(slot[:], slot[:], a[:], ALU.add))
            then(dve.tensor_tensor(slot[:], slot[:], spread(count[:], shape, 1), ALU.add))
            for k in range(K):
                then(dve.tensor_tensor(work[:], chosen[:, k], slot[:], ALU.mult))
                then(dve.tensor_reduce(pos[:, k], work[:], AX.X, ALU.add))
            then(dve.tensor_scalar(tile_of[:], pos[:], 1.0 / P, 0.5 / P - 0.5, ALU.mult, ALU.add))
            then(dve.tensor_scalar(tile_of[:], tile_of[:], ROUND, ROUND, ALU.add, ALU.subtract))
            then(dve.scalar_tensor_tensor(out=lane_of[:], in0=tile_of[:], scalar=-float(P), in1=pos[:], op0=ALU.mult, op1=ALU.add))
            flat = lambda t: t[:].rearrange("p k t -> p (k t)")
            dve.tensor_tensor(in_lane[:], spread(lane[:], [P, K * NT, P], 1), spread(flat(lane_of), [P, K * NT, P], 2), ALU.is_equal)
            then(dve.tensor_tensor(in_tile[:], spread(lane[:, 0:TILES], [P, K * NT, TILES], 1),
                                   spread(flat(tile_of), [P, K * NT, TILES], 2), ALU.is_equal))
            for k in range(K):
                half = slice(k * NT, (k + 1) * NT)
                dve.tensor_tensor(packed[:, half, 0], in_tile[:, half], spread(token[:], [P, NT, TILES], 2), ALU.mult)
            dve.tensor_tensor(packed[:, :, 1], in_tile[:], spread(flat(weight_hi), [P, K * NT, TILES], 2), ALU.mult)
            dve.tensor_tensor(packed[:, :, 2], in_tile[:], spread(flat(weight_lo), [P, K * NT, TILES], 2),
                              ALU.mult).then_inc(sem("packed"), 1)
            then(dve.tensor_tensor(ended[:], spread(c[:], [P, TILES, E], 1), spread(lane[:, 0:TILES], [P, TILES, E], 2), ALU.is_le))
            then(dve.tensor_reduce(expert_of[:], ended[:], AX.X, ALU.add))
            then(dve.tensor_scalar(expert_of[:], expert_of[:], float(E - 1), None, ALU.min))
            dve.tensor_scalar(gu_at[:], expert_of[:], float(C * 2 * F), None, ALU.mult).then_inc(sem("experts_known"), 1)
            dve.tensor_scalar(dn_at[:], expert_of[:], float(FC * D), None, ALU.mult).then_inc(sem("experts_known"), 1)
            dve.wait_ge(sem("sorted"), 1)
            then(dve.tensor_copy(table[:], bank_y[:, 0, 0:3 * TILES]))
            then(dve.tensor_scalar(unused[:], table[:, 0:TILES], 0.0, pad_row[:, 0:1], ALU.is_equal, ALU.mult))
            dve.scalar_tensor_tensor(out=gather_at[:], in0=table[:, 0:TILES], scalar=-1.0, in1=unused[:], op0=ALU.add,
                                     op1=ALU.add).then_inc(sem("gather_ready"), 1)
            then(dve.tensor_tensor(slot_weight[:], table[:, TILES:2 * TILES], table[:, 2 * TILES:], ALU.add))
            dve.tensor_scalar(slot_weight[:], slot_weight[:], 1.0 / (C_SCALE * A_SCALE), None, ALU.mult).then_inc(sem("weights_ready"), 1)

            def take_x(m, k):
                t = Tile(m, k)
                dve.wait_ge(sem("x_filled"), t.i + 1)
                if not (t.number is not None and t.number < 2):
                    dve.wait_ge(sem("gu_filled"), t.i - 1)
                dve.tensor_copy(xT[t.parity][:].rearrange("p h c t -> p (h c t)"),
                                bank_x[:, t.parity].bitcast(F16)).then_inc(sem("x_taken"), 1)

            def activate(m, k):
                t = Tile(m, k)
                dve.wait_ge(sem("gated"), t.i + 1)
                dve.scalar_tensor_tensor(out=gated[t.parity][:], in0=bank_gu[:, t.parity, F:2 * F], scalar=A_SCALE / X_SCALE,
                                         in1=gated[t.parity][:], op0=ALU.mult, op1=ALU.mult).then_inc(sem("gu_taken"), 1)
                dve.wait_ge(sem("act_hi"), t.i + 1)
                dve.tensor_tensor(act_hl[t.parity][:, 1], gated[t.parity][:], act_hl[t.parity][:, 0],
                                  ALU.subtract).then_inc(sem("act_lo"), 1)

            def step(m, k):
                t = Tile(m, k)
                if t.number is None or t.number < LAST:
                    take_x(m, k + 1)
                activate(m, k)

            take_x(0, 0)
            over_tiles(dve, step)

        @block.scalar
        def _(act):
            act.wait_ge(sem("shifted"), 1)
            act.activation(prob[:], work[:], ACT.Exp).then_inc(sem("exp_done"), 1)
            act.wait_ge(sem("weights_ready"), 1)

            def gate(m, k):
                t = Tile(m, k)
                act.wait_ge(sem("gu_filled"), t.i + 1)
                if not (t.number is not None and t.number < 2):
                    act.wait_ge(sem("act_lo"), t.i - 1)
                act.activation(gated[t.parity][:], bank_gu[:, t.parity, 0:F], ACT.Silu, scale=1.0 / X_SCALE).then_inc(sem("gated"), 1)
                act.wait_ge(sem("gu_taken"), t.i + 1)
                if not (t.number is not None and t.number < 2):
                    act.wait_ge(sem("a_filled"), t.i - 1)
                act.activation(act_hl[t.parity][:, 0], gated[t.parity][:], ACT.Copy).then_inc(sem("act_hi"), 1)

            def take_a(m, k):
                t = Tile(m, k)
                act.wait_ge(sem("a_filled"), t.i + 1)
                if not (t.number is not None and t.number < 2):
                    act.wait_ge(sem("y_filled"), t.i - 1)
                act.activation(aT[t.parity][:].rearrange("p h c t -> p (h c t)"),
                               bank_a[:, t.parity, 0:FC * P].bitcast(F16), ACT.Copy).then_inc(sem("a_taken"), 1)

            def take_y(m, k):
                t = Tile(m, k)
                act.wait_ge(sem("y_filled"), t.i + 1)
                if not (t.number is not None and t.number < 2):
                    act.wait_ge(sem("added"), 16 * (t.i - 1))
                act.activation(y[t.parity][:], bank_y[:, t.parity], ACT.Identity,
                               scale=t.column(slot_weight)).then_inc(sem("y_taken"), 1)

            def step(m, k):
                t = Tile(m, k)
                if t.number != 0:
                    take_a(m, k - 1)
                gate(m, k)
                if t.number != 0:
                    take_y(m, k - 1)

            over_tiles(act, step)
            take_a(0, LAST)
            take_y(0, LAST)

        @block.tensor
        def _(pe):
            pe.wait_ge(sem("mask_ready"), 1)
            flat_mask = mask[:].rearrange("p t e -> p (t e)")
            pe.matmul(bank_r[:, 0, 0:NT * E], below[:], flat_mask, start=True, stop=True)
            pe.matmul(bank_r[:, 1, 0:NT * E], onesb[:], flat_mask, start=True, stop=True).then_inc(sem("ranked"), 1)
            pe.wait_ge(sem("packed"), 1)
            for n in range(K * NT):
                ins = pe.matmul(bank_y[:, 0, 0:3 * TILES], in_lane[:, n], packed[:, n].rearrange("p k t -> p (k t)"),
                                start=(n == 0), stop=(n == K * NT - 1))
            ins.then_inc(sem("sorted"), 1)
            pe.wait_ge(sem("experts_known"), 2)
            pe.wait_ge(sem("weights_ready"), 1)

            def transpose_x(m, k):
                t = Tile(m, k)
                pe.wait_ge(sem(f"gathered{t.parity}"), 16 * (t.half + 1))
                if not (t.number is not None and t.number < 2):
                    pe.wait_ge(sem("x_taken"), t.i - 1)
                bank = bank_x[:, t.parity].bitcast(F16)
                for n in range(2 * C):
                    ins = pe.transpose(bank[:, n * P:(n + 1) * P], xg[t.parity][:, n * P:(n + 1) * P], identh[:])
                ins.then_inc(sem("x_filled"), 1)

            def gate_up(m, k, offset, chunks):
                t = Tile(m, k)
                if chunks[0] == 0:
                    pe.wait_ge(sem("x_taken"), t.i + 1)
                    if not (t.number is not None and t.number < 2):
                        pe.wait_ge(sem("gu_taken"), t.i - 1)
                for c in chunks:
                    cols = bass.ds(offset + c * 2 * F, 2 * F)
                    for n, (lhs, rhs) in enumerate(((0, gu_hi_at), (0, gu_lo_at), (1, gu_hi_at))):
                        ins = pe.matmul(bank_gu[:, t.parity], xT[t.parity][:, lhs, c], rhs[:, cols],
                                        start=(c == 0 and n == 0), stop=(c == C - 1 and n == 2))
                if chunks[-1] == C - 1:
                    ins.then_inc(sem("gu_filled"), 1)

            def transpose_a(m, k):
                t = Tile(m, k)
                pe.wait_ge(sem("act_lo"), t.i + 1)
                if not (t.number is not None and t.number < 2):
                    pe.wait_ge(sem("a_taken"), t.i - 1)
                bank = bank_a[:, t.parity].bitcast(F16)
                for n in range(2 * FC):
                    ins = pe.transpose(bank[:, n * P:(n + 1) * P], act_hl[t.parity][:, n // FC, n % FC * P:(n % FC + 1) * P], identh[:])
                ins.then_inc(sem("a_filled"), 1)

            def down(m, k, offset):
                t = Tile(m, k)
                pe.wait_ge(sem("a_taken"), t.i + 1)
                if not (t.number is not None and t.number < 2):
                    pe.wait_ge(sem("y_taken"), t.i - 1)
                for c in range(FC):
                    cols = bass.ds(offset + c * D, D)
                    for n, (lhs, rhs) in enumerate(((0, dn_hi_at), (0, dn_lo_at), (1, dn_hi_at))):
                        ins = pe.matmul(bank_y[:, t.parity], aT[t.parity][:, lhs, c], rhs[:, cols],
                                        start=(c == 0 and n == 0), stop=(c == FC - 1 and n == 2))
                ins.then_inc(sem("y_filled"), 1)

            def down_at(m, k):
                return pe.value_load(Tile(m, k).column(dn_at)[0:1], min_val=0, max_val=(E - 1) * FC * D)

            def step(m, k):
                t = Tile(m, k)
                if t.number is None or t.number < LAST:
                    transpose_x(m, k + 1)
                offset = pe.value_load(t.column(gu_at)[0:1], min_val=0, max_val=(E - 1) * C * 2 * F)
                gate_up(m, k, offset, range(0, C // 2))
                if t.number != 0:
                    down_offset = down_at(m, k - 1)
                    transpose_a(m, k - 1)
                gate_up(m, k, offset, range(C // 2, C))
                if t.number != 0:
                    down(m, k - 1, down_offset)

            transpose_x(0, 0)
            over_tiles(pe, step)
            transpose_a(0, LAST)
            down(0, LAST, down_at(0, LAST))


_INS = ["x", "fside_BxS2xS2_0", "ctx_1024", "L0_ffn_router_w", "L0_ffn_gate_proj", "L0_ffn_up_proj", "L0_ffn_down_proj"]


def kernel(**inputs):
    import numpy as np
    import concourse.bacc as bacc
    from concourse.bass_utils import run_bass_kernel_spmd

    nc = bacc.Bacc("TRN2", target_bir_lowering=False, num_devices=1)
    arrays, args = {}, []
    for name in _INS:
        a = np.ascontiguousarray(inputs[name])
        arrays[f"in_{name}"] = a
        args.append(nc.dram_tensor(f"in_{name}", a.shape, mybir.dt.from_np(a.dtype), kind="ExternalInput").ap())
    B, T, D = arrays["in_x"].shape
    args.append(nc.dram_tensor("out", (B * T + P, D), F32, kind="ExternalOutput").ap())
    block_kernel(nc, *args)
    result = run_bass_kernel_spmd(nc, [arrays], core_ids=[0]).results[0]["out"]
    return result[:B * T].reshape(B, T, D)
```

```python
from contextlib import ExitStack
from functools import partial

import concourse.bass as bass
from concourse import mybir

F32 = mybir.dt.float32
F16 = mybir.dt.float16
BF16 = mybir.dt.bfloat16
I32 = mybir.dt.int32
ALU = mybir.AluOpType
ACT = mybir.ActivationFunctionType
AX = mybir.AxisListType

P = 128
LN_EPS = 1e-5
EPS = 1e-6
QMAX = 127.0
ROUND = 12582912.0
X_SCALE = 256.0
A_SCALE = 16.0
C_SCALE = 1024.0


SP_ORDER = ["load x", "load expert 0", "load expert 1", "load w1", "store x1", "load expert 2", "load expert 3",
            "load expert 4", "store halves", "load expert 5", "load x again", "load w2"]
POOL_ORDER = ["deviation 2", "deviation 1", "low 0", "low 1", "low half", "root 2", "low 2", "root 1", "smooth w2", "low 3",
              "smooth w1", "low 4", "residual", "low 5"]
DVE_ORDER = ["moments 2", "moments 1", "shift 2", "product 1", "w2 columns", "gate times up", "shift 1", "a columns",
             "ratio 2", "w1 columns", "smoothing 2", "x columns", "ratio 1", "smooth a", "smoothing 1", "a scales",
             "smooth x", "w2 scales", "x scales", "w1 scales", "product 2"]
ACT_ORDER = ["high 0", "high 1", "normalise 2", "silu", "high half", "tokens B", "normalise 1", "high 2", "tokens A",
             "rows 2", "high 3", "rows 1", "a up", "high 4", "scores B", "high 5", "scores A", "w2 up", "a transposed",
             "w2 scale row", "w2 transposed", "x up", "w1 up", "x transposed", "w1 transposed", "w1 scale row"]
PE_ORDER = ["product 1", "w2 columns", "tokens B", "a columns", "tokens A", "w1 columns", "x columns", "rows 2",
            "scores B", "rows 1", "scores A", "a transposed", "w2 scale row", "w2 transposed", "product 2", "x transposed",
            "w1 transposed", "w1 scale row"]
TWO_AHEAD = {
    "load x", "load w1", "load w2", "load expert 0", "high 0", "low 0", "load expert 1", "high 1", "low 1",
    "load expert 2", "high 2", "low 2", "load expert 3", "high 3", "low 3", "load expert 4", "high 4", "low 4",
    "load expert 5", "high 5", "low 5", "moments 1", "deviation 1", "shift 1", "normalise 1", "w1 columns",
    "x columns", "ratio 1", "root 1", "smoothing 1", "rows 1", "smooth x", "x scales", "smooth w1",
    "w1 scales", "x up", "w1 up", "x transposed", "w1 transposed", "w1 scale row"}
ONE_AHEAD = {
    "load x again", "product 1", "silu", "gate times up", "a columns", "w2 columns", "ratio 2", "root 2",
    "smoothing 2", "rows 2", "smooth a", "a scales", "smooth w2", "w2 scales", "a up", "w2 up", "a transposed",
    "w2 transposed", "w2 scale row", "product 2", "residual"}
AHEAD = 2


def ahead(stage):
    return 2 if stage in TWO_AHEAD else 1 if stage in ONE_AHEAD else 0


class Signals:

    def __init__(self, nc, ctx):
        self.nc, self.ctx, self.made = nc, ctx, {}

    def __call__(self, name):
        if name not in self.made:
            self.made[name] = self.ctx.enter_context(self.nc.semaphore(name))
        return self.made[name]


class Ring:

    def __init__(self, psum, filled, taken, batches, order, taker_orders, uses):
        self.psum, self.filled, self.taken, self.batches, self.uses = psum, filled, taken, batches, uses
        self.order = [name for name in order if name in uses]
        assert sum(uses.values()) % 2 == 0
        for other in taker_orders:
            assert [name for name in other if name in uses] == self.order

    def sum_of(self, names):
        return sum(self.uses[name] for name in names)

    def before(self, stage, u, b):
        i = b - ahead(stage)
        now = self.order[:self.order.index(stage)]
        if isinstance(b, int):
            n = sum(self.uses[name] * min(max(i + ahead(name), 0), self.batches) for name in self.order)
            n += self.sum_of(name for name in now if 0 <= i + ahead(name) < self.batches) + u
            return n, n % 2
        ahead_of_it = sum(self.uses[name] * ahead(name) for name in self.order) + self.sum_of(now) + u
        return i * self.sum_of(self.order) + ahead_of_it, ahead_of_it % 2

    def fill(self, pe, stage, u, b):
        n, bank = self.before(stage, u, b)
        if not (isinstance(n, int) and n < 2):
            pe.wait_ge(self.taken, n - 1)
        return self.psum[:, bank]

    def empty(self, eng, stage, u, b):
        n, bank = self.before(stage, u, b)
        eng.wait_ge(self.filled, n + 1)
        return self.psum[:, bank]

    def emptied(self, eng, stage, u, b):
        eng.wait_ge(self.taken, self.before(stage, u, b)[0] + 1)


def upto(b, per_batch, j=None):
    return b * per_batch + (per_batch if j is None else j + 1)


def is_first(b):
    return isinstance(b, int) and b == 0


def block_kernel(nc, x, w1, w2, router_w, gate_w, up_w, down_w, out):
    B, T, D = x.shape
    O1 = w1.shape[1]
    I = w2.shape[2]
    E, _, F = gate_w.shape
    J = T // P
    C = D // P
    IC = I // P
    FC = F // P
    NT = B * J
    N = B * T
    TOPK = 2
    TILES = (N * TOPK + E * (P - 1)) // P
    EPB = E // B
    PPB = 3 * EPB
    assert TILES % 2 == 1 and O1 == T == D and 2 * I == O1 and C * F == FC * D

    halves_dram = nc.dram_tensor("token_halves", (N + P, 2 * D), F16).ap()

    with ExitStack() as ctx:
        def sb(name, shape, dt):
            return ctx.enter_context(nc.sbuf_tensor(name, shape, dt))

        def ps(name):
            return ctx.enter_context(nc.psum_tensor(name, [P, 2, 512], F32))

        sem = Signals(nc, ctx)

        gu_hi = sb("gu_hi", [P, E, C, 2 * F], F16)
        gu_lo = sb("gu_lo", [P, E, C, 2 * F], BF16)
        dn_hi = sb("dn_hi", [P, E, FC, D], F16)
        dn_lo = sb("dn_lo", [P, E, FC, D], BF16)
        identf = sb("identf", [P, P], F32)
        identh = sb("identh", [P, P], F16)
        below = sb("below", [P, P], BF16)
        onesb = sb("onesb", [P, P], BF16)
        power = sb("power", [P, 2, C], F32)
        rw = sb("rw", [P, C, E], F32)
        scores = sb("scores", [P, NT, E], F32)
        gather_at = sb("gather_at", [P, TILES], I32)
        slot_weight = sb("slot_weight", [P, TILES], F32)
        gu_at = sb("gu_at", [P, TILES], I32)
        dn_at = sb("dn_at", [P, TILES], I32)

        bank_t, bank_r, bank_q, bank_h = ps("bank_t"), ps("bank_r"), ps("bank_q"), ps("bank_h")

        hold_p = sb("hold_p", [P, 1], F32)
        hold_v = sb("hold_v", [P, 1], F32)

        def hold(pool):
            pool.tensor_tensor(hold_p[:], identf[:, 0:1], identf[:, 0:1], ALU.add)

        def spread(ap, shape, axis):
            return ap.unsqueeze(axis).to_broadcast(shape)

        def at(t, b):
            return t[:, b] if isinstance(b, int) else t[:, bass.ds(b, 1)].squeeze(1)

        def row_of(t, b):
            return t[b] if isinstance(b, int) else t[bass.ds(b, 1)].squeeze(0)

        zeros = sb("zeros", [P, D], F32)

        part1 = ExitStack()

        def tmp(name, shape, dt):
            return part1.enter_context(nc.sbuf_tensor(name, shape, dt))

        x_in = tmp("x_in", [P, J, D], F32)
        w1_in = tmp("w1_in", [P, J, D], F32)
        w2_in = tmp("w2_in", [P, J, I], F32)
        xn = tmp("xn", [P, J, D], F32)
        rows1 = tmp("rows1", [P, 3, D], F32)
        h = tmp("h", [P, J, O1], F32)
        xqT = tmp("xqT", [P, C, T], BF16)
        wqT = tmp("wqT", [P, C, O1], BF16)
        av = tmp("av", [P, J, I], F32)
        rows2 = tmp("rows2", [P, 2, I], F32)
        row_w2 = tmp("row_w2", [P, D], F32)
        aqT = tmp("aqT", [P, IC, T], BF16)
        dqT = tmp("dqT", [P, IC, D], BF16)
        x1 = tmp("x1", [P, J, D], F32)
        xn2 = tmp("xn2", [P, J, D], F32)
        halves = tmp("halves", [P, J, 2, D], F16)
        xn2T = tmp("xn2T", [P, 2, 2, D], F32)
        stage = tmp("stage", [P, 3, C * F], F32)
        stats = tmp("stats", [P, 2, J, 6], F32)
        mv = tmp("mv", [P, 2, J, 2], F32)
        rstd = tmp("rstd", [P, 2, J], F32)
        shift = tmp("shift", [P, 2, J], F32)
        amax = [tmp(f"amax{k}", [P, 2, n], F32) for k, n in ((0, C), (1, IC))]
        ratio = [tmp(f"ratio{k}", [P, n], F32) for k, n in ((0, C), (1, IC))]
        smooth = [tmp(f"smooth{k}", [P, 2, n], F32) for k, n in ((0, C), (1, IC))]
        rmax = tmp("rmax", [P, 2, 2, J], F32)
        scale = tmp("scale", [P, 2, 2, J], F32)
        inv = tmp("inv", [P, 2, 2, J], F32)

        x_dram = x.rearrange("b (p j) d -> b p j d", j=J)
        out_dram = out[0:N].rearrange("(b p j) d -> b p j d", b=B, j=J)
        halves_out = halves_dram[0:N].rearrange("(b p j) d -> b p (j d)", b=B, j=J)
        w1_dram = w1.rearrange("b (j p) d -> b p j d", p=P)
        w2_dram = w2.rearrange("b (j p) i -> b p j i", p=P)
        expert_dram = (gate_w.rearrange("e (c p) f -> e p c f", p=P), up_w.rearrange("e (c p) f -> e p c f", p=P),
                       down_w.rearrange("e (c p) d -> e p c d", p=P))

        def staged(m):
            return stage[:, m % 3].rearrange("p (c f) -> p c f", c=C if m % 3 < 2 else FC)

        def parts(b, m):
            e = b * EPB + m // 3
            if m % 3 < 2:
                cols = slice(m % 3 * F, (m % 3 + 1) * F)
                return at(gu_hi, e)[:, :, cols], at(gu_lo, e)[:, :, cols]
            return at(dn_hi, e), at(dn_lo, e)

        ring_t = Ring(bank_t, sem("t_filled"), sem("t_taken"), B, PE_ORDER, (DVE_ORDER,),
                      {"w1 columns": C, "x columns": C, "w2 columns": IC, "a columns": IC})
        ring_r = Ring(bank_r, sem("r_filled"), sem("r_taken"), B, PE_ORDER, (ACT_ORDER,),
                      {"rows 1": 2, "w1 scale row": 1, "rows 2": 2, "w2 scale row": 1})
        ring_q = Ring(bank_q, sem("q_filled"), sem("q_taken"), B, PE_ORDER, (ACT_ORDER,),
                      {"x transposed": C, "w1 transposed": C, "a transposed": IC, "w2 transposed": IC,
                       "tokens A": 2, "tokens B": 2, "scores A": 1, "scores B": 1})
        ring_h = Ring(bank_h, sem("h_filled"), sem("h_taken"), B, PE_ORDER, (DVE_ORDER,), {"product 1": J, "product 2": J})

        def woven(eng, order, steps):
            assert set(order) == set(steps)

            def run(i):
                for name in order:
                    b = i + ahead(name)
                    if not isinstance(b, int) or 0 <= b < B:
                        steps[name](b)

            for i in range(-AHEAD, 1):
                run(i)
            with eng.Fori(1, B - AHEAD) as i:
                run(i)
            for i in range(B - AHEAD, B):
                run(i)

        block = part1.enter_context(nc.Block())

        @block.sync
        def _(sp):
            sp.dma_start(rw[:], router_w.rearrange("(c p) e -> p c e", p=P)).then_inc(sem("router_in"), 16)

            def load_x(b):
                if not is_first(b):
                    sp.wait_ge(sem("xn_ready"), upto(b, J) - J)
                sp.dma_start(x_in[:], row_of(x_dram, b)).then_inc(sem("x_in"), 16)

            def load_w1(b):
                if not is_first(b):
                    sp.wait_ge(ring_q.filled, ring_q.before("w1 transposed", C - 1, b - 1)[0] + 1)
                sp.dma_start(w1_in[:], row_of(w1_dram, b)).then_inc(sem("w1_in"), 16)

            def load_w2(b):
                if not is_first(b):
                    sp.wait_ge(ring_q.filled, ring_q.before("w2 transposed", IC - 1, b - 1)[0] + 1)
                sp.dma_start(w2_in[:], row_of(w2_dram, b)).then_inc(sem("w2_in"), 16)

            def load_x_again(b):
                if not is_first(b):
                    stored = 16 * (upto(b, 1) - 1)
                    sp.wait_ge(sem("x1_stored"), stored)
                    sp.wait_ge(sem("halves_stored"), stored)
                sp.dma_start(x1[:], row_of(x_dram, b)).then_inc(sem("x_again"), 16)

            def load_expert(m, b):
                if not (is_first(b) and m < 3):
                    sp.wait_ge(sem("lo_done"), upto(b, PPB, m) - 3)
                sp.dma_start(staged(m), row_of(expert_dram[m % 3], b * EPB + m // 3)).then_inc(sem(f"stage_in{m % 3}"), 16)

            def store_x1(b):
                sp.wait_ge(sem("x1_ready"), upto(b, J))
                sp.dma_start(row_of(out_dram, b), x1[:]).then_inc(sem("x1_stored"), 16)

            def store_halves(b):
                sp.wait_ge(sem("hi_half"), upto(b, 1))
                sp.wait_ge(sem("lo_half"), upto(b, 1))
                sp.dma_start(row_of(halves_out, b), halves[:].rearrange("p j k d -> p (j k d)")).then_inc(sem("halves_stored"), 16)

            woven(sp, SP_ORDER,
                  {"load x": load_x, "load w1": load_w1, "load w2": load_w2, "load x again": load_x_again,
                   "store x1": store_x1, "store halves": store_halves,
                   **{f"load expert {m}": partial(load_expert, m) for m in range(PPB)}})
            sp.wait_ge(sem("zeroed"), 1)
            sp.dma_start(out[N:N + P], zeros[:]).then_inc(sem("pad_stored"), 16)
            sp.dma_start(halves_dram[N:N + P], zeros[:].bitcast(F16)).then_inc(sem("pad_stored"), 16)
            sp.wait_ge(sem("router_in"), 16)

        @block.gpsimd
        def _(pool):
            pool.memset(identf[:], 0.0).then_inc(sem("blank"), 1)
            pool.memset(below[:], 1.0).then_inc(sem("blank"), 1)
            pool.memset(power[:, 0], -0.5).then_inc(sem("constants"), 1)
            pool.memset(power[:, 1], 0.5).then_inc(sem("constants"), 1)
            pool.wait_ge(sem("blank"), 2)
            pool.affine_select(out=identf[:], in_=identf[:], compare_op=ALU.not_equal, fill=1.0, base=0,
                               pattern=[[-1, P]], channel_multiplier=1).then_inc(sem("constants"), 1)
            pool.affine_select(out=below[:], in_=below[:], compare_op=ALU.is_gt, fill=0.0, base=0,
                               pattern=[[1, P]], channel_multiplier=-1).then_inc(sem("constants"), 1)
            pool.wait_ge(sem("constants"), 4)
            pool.tensor_copy(identh[:], identf[:]).then_inc(sem("idents"), 1)
            pool.memset(onesb[:], 1.0).then_inc(sem("constants"), 1)
            pool.memset(zeros[:], 0.0).then_inc(sem("zeroed"), 1)

            def low(m, b):
                hi, lo = parts(b, m)
                pool.wait_ge(sem("hi_done"), upto(b, PPB, m))
                pool.tensor_tensor(lo, staged(m), hi, ALU.subtract).then_inc(sem("lo_done"), 1)

            def root(out_ap, in_ap, which, ready, done, b):
                pool.wait_ge(ready, upto(b, 1))
                pool.tensor_tensor(out_ap, in_ap, power[:, which, 0:in_ap.shape[1]], ALU.pow).then_inc(done, 1)

            def deviation(which, b):
                root(rstd[:, which], mv[:, which, :, 1], 0, sem(f"var{which}"), sem(f"rstd{which}"), b)

            def smoothing_root(which, b):
                root(smooth[which][:, 1], ratio[which][:], 1, sem(f"ratio{which}"), sem(f"root{which}"), b)

            def smooth_w1(b):
                ring_r.emptied(pool, "rows 1", 1, b)
                for j in range(0, J, J // 2):
                    rows = w1_in[:, j:j + J // 2]
                    pool.tensor_tensor(rows, rows, spread(rows1[:, 1], [P, J // 2, D], 1), ALU.mult).then_inc(sem("ws_ready"), 1)

            def smooth_w2(b):
                ring_r.emptied(pool, "rows 2", 1, b)
                pool.tensor_tensor(w2_in[:], w2_in[:], spread(rows2[:, 1], [P, J, I], 1), ALU.mult).then_inc(sem("ds_ready"), 1)

            def residual(b):
                pool.wait_ge(sem("x_again"), 16 * upto(b, 1))
                for j in range(J):
                    ring_h.emptied(pool, "product 2", j, b)
                    pool.tensor_tensor(x1[:, j], x1[:, j], xn2[:, j], ALU.add).then_inc(sem("x1_ready"), 1)

            def low_half(b):
                pool.wait_ge(sem("xn2_ready"), upto(b, J))
                pool.wait_ge(sem("hi_half"), upto(b, 1))
                if not is_first(b):
                    pool.wait_ge(sem("halves_stored"), 16 * (upto(b, 1) - 1))
                pool.tensor_tensor(halves[:, :, 1], xn2[:], halves[:, :, 0], ALU.subtract).then_inc(sem("lo_half"), 1)

            woven(pool, POOL_ORDER,
                  {"deviation 1": partial(deviation, 0), "root 1": partial(smoothing_root, 0), "smooth w1": smooth_w1,
                   "root 2": partial(smoothing_root, 1), "smooth w2": smooth_w2, "residual": residual,
                   "deviation 2": partial(deviation, 1), "low half": low_half,
                   **{f"low {m}": partial(low, m) for m in range(PPB)}})

        @block.vector
        def _(dve):
            def moments(b, which, src, ready, per_batch):
                for j in range(J):
                    if j < per_batch:
                        dve.wait_ge(ready, upto(b, per_batch, j) * (16 if per_batch == 1 else 1))
                    dve.bn_stats(stats[:, which, j], src[:, j]).then_inc(sem(f"stats{which}"), 1)
                dve.wait_ge(sem(f"stats{which}"), upto(b, J))
                dve.tensor_copy(hold_v[:], stats[:, which, 0, 0:1])
                for j in range(J):
                    dve.bn_aggr(mv[:, which, j], stats[:, which, j]).then_inc(sem(f"moments{which}"), 1)
                dve.wait_ge(sem(f"moments{which}"), upto(b, J))
                dve.tensor_scalar(mv[:, which, :, 1], mv[:, which, :, 1], LN_EPS, None, ALU.add).then_inc(sem(f"var{which}"), 1)

            def shift_of(which):
                dve.scalar_tensor_tensor(out=shift[:, which], in0=mv[:, which, :, 0], scalar=-1.0, in1=rstd[:, which],
                                         op0=ALU.mult, op1=ALU.mult).then_inc(sem(f"shift{which}"), 1)

            def shift1(b):
                dve.wait_ge(sem("rstd0"), upto(b, 1))
                shift_of(0)

            def shift2(b):
                dve.wait_ge(sem("rstd1"), upto(b, 1))
                dve.tensor_scalar(rstd[:, 1], rstd[:, 1], X_SCALE, None, ALU.mult).then_inc(sem("rstd1_scaled"), 1)
                dve.wait_ge(sem("rstd1_scaled"), upto(b, 1))
                shift_of(1)

            def column_max(stage, dst, chunks, b):
                for c in range(chunks):
                    bank = ring_t.empty(dve, stage, c, b)
                    dve.tensor_reduce(dst[:, c:c + 1], bank, AX.X, ALU.max,
                                      apply_absolute_value=True).then_inc(ring_t.taken, 1)

            def smoothing_ratio(which, last_stages, b):
                done = sem(f"clamped{which}")
                for stage in last_stages:
                    ring_t.emptied(dve, stage, amax[which].shape[2] - 1, b)
                dve.tensor_scalar(amax[which][:], amax[which][:], EPS, None, ALU.max).then_inc(done, 1)
                dve.wait_ge(done, upto(b, 2, 0))
                dve.reciprocal(ratio[which][:], amax[which][:, 1]).then_inc(done, 1)
                dve.wait_ge(done, upto(b, 2, 1))
                dve.tensor_tensor(ratio[which][:], ratio[which][:], amax[which][:, 0], ALU.mult).then_inc(sem(f"ratio{which}"), 1)

            def smoothing(which, b):
                done = sem(f"smooth{which}")
                dve.wait_ge(sem(f"root{which}"), upto(b, 1))
                dve.tensor_scalar(smooth[which][:, 1], smooth[which][:, 1], EPS, None, ALU.max).then_inc(done, 1)
                dve.wait_ge(done, upto(b, 2, 0))
                dve.reciprocal(smooth[which][:, 0], smooth[which][:, 1]).then_inc(done, 1)

            def row_scales(which, side, src, ready, cuts, b):
                done = sem(f"row_max{which}{side}")
                for n in range(cuts):
                    rows = slice(n * J // cuts, (n + 1) * J // cuts)
                    dve.wait_ge(ready, upto(b, cuts, n))
                    dve.tensor_reduce(rmax[:, which, side, rows], src[:, rows], AX.X, ALU.max, apply_absolute_value=True).then_inc(done, 1)
                    dve.wait_ge(done, upto(b, 2 * cuts, 2 * n))
                    dve.tensor_scalar(scale[:, which, side, rows], rmax[:, which, side, rows], EPS, 1.0 / QMAX, ALU.max,
                                      ALU.mult).then_inc(done, 1)
                    dve.wait_ge(done, upto(b, 2 * cuts, 2 * n + 1))
                    dve.reciprocal(inv[:, which, side, rows], scale[:, which, side, rows]).then_inc(sem(f"inv{which}{side}"), 1)

            def smooth_x(b):
                ring_r.emptied(dve, "rows 1", 0, b)
                for j in range(0, J, J // 2):
                    rows = xn[:, j:j + J // 2]
                    dve.tensor_tensor(rows, rows, spread(rows1[:, 0], [P, J // 2, D], 1), ALU.mult).then_inc(sem("xs_ready"), 1)

            def smooth_a(b):
                ring_r.emptied(dve, "rows 2", 0, b)
                dve.tensor_tensor(av[:], av[:], spread(rows2[:, 0], [P, J, I], 1), ALU.mult).then_inc(sem("as_ready"), 1)

            def product1(b):
                ring_r.emptied(dve, "w1 scale row", 0, b)
                if not is_first(b):
                    dve.wait_ge(sem("silu_done"), upto(b, 1) - 1)
                for j in range(J):
                    bank = ring_h.empty(dve, "product 1", j, b)
                    dve.scalar_tensor_tensor(out=h[:, j], in0=bank, scalar=scale[:, 0, 0, j:j + 1], in1=rows1[:, 2],
                                             op0=ALU.mult, op1=ALU.mult).then_inc(ring_h.taken, 1)

            def gate_times_up(b):
                dve.wait_ge(sem("silu_done"), upto(b, 1))
                dve.tensor_tensor(av[:], av[:], h[:, :, I:2 * I], ALU.mult).then_inc(sem("a_ready"), 1)

            def product2(b):
                ring_r.emptied(dve, "w2 scale row", 0, b)
                if not is_first(b):
                    dve.wait_ge(sem("lo_half"), upto(b, 1) - 1)
                    ring_q.emptied(dve, "tokens A", 1, b - 1)
                    ring_q.emptied(dve, "tokens B", 1, b - 1)
                for j in range(J):
                    bank = ring_h.empty(dve, "product 2", j, b)
                    dve.scalar_tensor_tensor(out=xn2[:, j], in0=bank, scalar=scale[:, 1, 0, j:j + 1], in1=row_w2[:],
                                             op0=ALU.mult, op1=ALU.mult).then_inc(ring_h.taken, 1)

            woven(dve, DVE_ORDER,
                  {"moments 1": lambda b: moments(b, 0, x_in, sem("x_in"), 1), "shift 1": shift1,
                   "w1 columns": partial(column_max, "w1 columns", amax[0][:, 1], C),
                   "x columns": partial(column_max, "x columns", amax[0][:, 0], C),
                   "ratio 1": partial(smoothing_ratio, 0, ("w1 columns", "x columns")),
                   "smoothing 1": partial(smoothing, 0), "smooth x": smooth_x,
                   "x scales": partial(row_scales, 0, 0, xn[:], sem("xs_ready"), 2),
                   "w1 scales": partial(row_scales, 0, 1, w1_in[:], sem("ws_ready"), 2),
                   "product 1": product1, "gate times up": gate_times_up,
                   "w2 columns": partial(column_max, "w2 columns", amax[1][:, 1], IC),
                   "a columns": partial(column_max, "a columns", amax[1][:, 0], IC),
                   "ratio 2": partial(smoothing_ratio, 1, ("w2 columns", "a columns")),
                   "smoothing 2": partial(smoothing, 1), "smooth a": smooth_a,
                   "a scales": partial(row_scales, 1, 0, av[:], sem("as_ready"), 1),
                   "w2 scales": partial(row_scales, 1, 1, w2_in[:], sem("ds_ready"), 1),
                   "product 2": product2, "moments 2": lambda b: moments(b, 1, x1, sem("x1_ready"), J), "shift 2": shift2})

        @block.scalar
        def _(act):
            def normalise(b, which, src, dst, done):
                act.wait_ge(sem(f"shift{which}"), upto(b, 1))
                for j in range(J):
                    act.activation(dst[:, j], src[:, j], ACT.Identity, bias=shift[:, which, j:j + 1],
                                   scale=rstd[:, which, j:j + 1]).then_inc(done, 1)

            def normalise1(b):
                if not is_first(b):
                    act.wait_ge(ring_q.filled, ring_q.before("x transposed", C - 1, b - 1)[0] + 1)
                normalise(b, 0, x_in, xn, sem("xn_ready"))

            def take_row(stage, u, b, dst):
                bank = ring_r.empty(act, stage, u, b)
                act.activation(dst, bank[:, 0:dst.shape[1]], ACT.Copy).then_inc(ring_r.taken, 1)

            def smoothing_rows(stage, users, dst, b):
                if not is_first(b):
                    for name, per_batch in users:
                        act.wait_ge(sem(name), upto(b, per_batch) - per_batch)
                take_row(stage, 0, b, dst[:, 0])
                take_row(stage, 1, b, dst[:, 1])

            def scale_row(stage, product, dst, b):
                if not is_first(b):
                    ring_h.emptied(act, product, J - 1, b - 1)
                take_row(stage, 0, b, dst)

            def scale_up(which, side, t, cuts, done, b):
                for j in range(J):
                    if j % (J // cuts) == 0:
                        act.wait_ge(sem(f"inv{which}{side}"), upto(b, cuts, j * cuts // J))
                    ins = act.activation(t[:, j], t[:, j], ACT.Identity, bias=ROUND, scale=inv[:, which, side, j:j + 1])
                ins.then_inc(done, 1)

            def take_transposed(stage, dst, chunks, product, b):
                if not is_first(b):
                    act.wait_ge(ring_h.filled, ring_h.before(product, J - 1, b - 1)[0] + 1)
                for c in range(chunks):
                    bank = ring_q.empty(act, stage, c, b)
                    act.activation(dst[:, c], bank, ACT.Identity, bias=-ROUND).then_inc(ring_q.taken, 1)

            def high(m, b):
                hi, _ = parts(b, m)
                act.wait_ge(sem(f"stage_in{m % 3}"), 16 * upto(b, EPB, m // 3))
                act.activation(hi, staged(m), ACT.Copy).then_inc(sem("hi_done"), 1)

            def silu(b):
                if not is_first(b):
                    act.wait_ge(ring_q.filled, ring_q.before("a transposed", IC - 1, b - 1)[0] + 1)
                ring_h.emptied(act, "product 1", J - 1, b)
                act.activation(av[:], h[:, :, 0:I], ACT.Silu).then_inc(sem("silu_done"), 1)

            def high_half(b):
                act.wait_ge(sem("xn2_ready"), upto(b, J))
                if not is_first(b):
                    act.wait_ge(sem("halves_stored"), 16 * (upto(b, 1) - 1))
                act.activation(halves[:, :, 0], xn2[:], ACT.Copy).then_inc(sem("hi_half"), 1)

            def take_tokens(stage, pair, b):
                for j in range(2):
                    bank = ring_q.empty(act, stage, j, b)
                    act.activation(xn2T[:, pair, j], bank, ACT.Copy).then_inc(ring_q.taken, 1)

            def take_scores(stage, pair, b):
                bank = ring_q.empty(act, stage, 0, b)
                tile = b * J + 2 * pair
                dst = scores[:, tile:tile + 2] if isinstance(b, int) else scores[:, bass.ds(tile, 2)]
                act.activation(dst, bank[:, 0:2 * E].rearrange("p (j e) -> p j e", e=E), ACT.Copy,
                               scale=1.0 / X_SCALE).then_inc(ring_q.taken, 1)

            woven(act, ACT_ORDER,
                  {"normalise 1": normalise1, "rows 1": partial(smoothing_rows, "rows 1", (("xs_ready", 2), ("ws_ready", 2)), rows1),
                   "x up": partial(scale_up, 0, 0, xn, 2, sem("xq_up")), "w1 up": partial(scale_up, 0, 1, w1_in, 2, sem("wq_up")),
                   "x transposed": partial(take_transposed, "x transposed", xqT, C, "product 1"),
                   "w1 transposed": partial(take_transposed, "w1 transposed", wqT, C, "product 1"),
                   "w1 scale row": partial(scale_row, "w1 scale row", "product 1", rows1[:, 2]), "silu": silu,
                   "rows 2": partial(smoothing_rows, "rows 2", (("as_ready", 1), ("ds_ready", 1)), rows2),
                   "a up": partial(scale_up, 1, 0, av, 1, sem("aq_up")), "w2 up": partial(scale_up, 1, 1, w2_in, 1, sem("dq_up")),
                   "a transposed": partial(take_transposed, "a transposed", aqT, IC, "product 2"),
                   "w2 transposed": partial(take_transposed, "w2 transposed", dqT, IC, "product 2"),
                   "w2 scale row": partial(scale_row, "w2 scale row", "product 2", row_w2[:]),
                   "normalise 2": lambda b: normalise(b, 1, x1, xn2, sem("xn2_ready")), "high half": high_half,
                   "tokens A": partial(take_tokens, "tokens A", 0), "tokens B": partial(take_tokens, "tokens B", 1),
                   "scores A": partial(take_scores, "scores A", 0), "scores B": partial(take_scores, "scores B", 1),
                   **{f"high {m}": partial(high, m) for m in range(PPB)}})

        @block.tensor
        def _(pe):
            pe.wait_ge(sem("constants"), 4)
            pe.wait_ge(sem("idents"), 1)
            pe.wait_ge(sem("router_in"), 16)

            def transposed(ring, stage, src, chunks, ready, per_batch, b):
                pe.wait_ge(ready, upto(b, per_batch))
                for c in range(chunks):
                    bank = ring.fill(pe, stage, c, b)
                    for j in range(J):
                        ins = pe.transpose(bank[:, j * P:(j + 1) * P], src[:, j, c * P:(c + 1) * P], identf[:])
                    ins.then_inc(ring.filled, 1)

            def as_row(stage, u, b, columns):
                bank = ring_r.fill(pe, stage, u, b)
                n = columns.shape[1]
                for c in range(n):
                    ins = pe.transpose(bank[:, c * P:(c + 1) * P], columns[:, c:c + 1].to_broadcast([P, P]), identf[:])
                ins.then_inc(ring_r.filled, 1)

            def smoothing_rows(stage, which, b):
                pe.wait_ge(sem(f"smooth{which}"), upto(b, 2))
                as_row(stage, 0, b, smooth[which][:, 0])
                as_row(stage, 1, b, smooth[which][:, 1])

            def scale_row(stage, which, cuts, b):
                pe.wait_ge(sem(f"inv{which}1"), upto(b, cuts))
                as_row(stage, 0, b, scale[:, which, 1])

            def product(stage, lhs, rhs, sources, b):
                for source in sources:
                    ring_q.emptied(pe, source, lhs.shape[1] - 1, b)
                for j in range(J):
                    bank = ring_h.fill(pe, stage, j, b)
                    for c in range(lhs.shape[1]):
                        ins = pe.matmul(bank, lhs[:, c, j * P:(j + 1) * P], rhs[:, c], start=(c == 0), stop=(c == lhs.shape[1] - 1))
                    ins.then_inc(ring_h.filled, 1)

            def tokens(stage, pair, b):
                pe.wait_ge(sem("xn2_ready"), upto(b, J, 2 * pair + 1))
                for j in range(2):
                    bank = ring_q.fill(pe, stage, j, b)
                    for c in range(C):
                        ins = pe.transpose(bank[:, c * P:(c + 1) * P], xn2[:, 2 * pair + j, c * P:(c + 1) * P], identf[:])
                    ins.then_inc(ring_q.filled, 1)

            def router(stage, pair, source, b):
                ring_q.emptied(pe, source, 1, b)
                bank = ring_q.fill(pe, stage, 0, b)
                for j in range(2):
                    for c in range(C):
                        ins = pe.matmul(bank[:, j * E:(j + 1) * E], xn2T[:, pair, j, c * P:(c + 1) * P], rw[:, c],
                                        start=(c == 0), stop=(c == C - 1))
                ins.then_inc(ring_q.filled, 1)

            def columns(stage, src, chunks, ready, per_batch):
                return partial(transposed, ring_t, stage, src, chunks, ready, per_batch)

            def quantised(stage, src, chunks, ready):
                return partial(transposed, ring_q, stage, src, chunks, ready, 1)

            def loaded(stage, src, chunks, ready):
                def run(b):
                    pe.wait_ge(ready, 16 * upto(b, 1))
                    for c in range(chunks):
                        bank = ring_t.fill(pe, stage, c, b)
                        for j in range(J):
                            ins = pe.transpose(bank[:, j * P:(j + 1) * P], src[:, j, c * P:(c + 1) * P], identf[:])
                        ins.then_inc(ring_t.filled, 1)
                return run

            woven(pe, PE_ORDER,
                  {"w1 columns": loaded("w1 columns", w1_in, C, sem("w1_in")),
                   "x columns": columns("x columns", xn, C, sem("xn_ready"), J),
                   "rows 1": partial(smoothing_rows, "rows 1", 0),
                   "x transposed": quantised("x transposed", xn, C, sem("xq_up")),
                   "w1 transposed": quantised("w1 transposed", w1_in, C, sem("wq_up")),
                   "w1 scale row": partial(scale_row, "w1 scale row", 0, 2),
                   "product 1": partial(product, "product 1", xqT, wqT, ("x transposed", "w1 transposed")),
                   "w2 columns": loaded("w2 columns", w2_in, IC, sem("w2_in")),
                   "a columns": columns("a columns", av, IC, sem("a_ready"), 1),
                   "rows 2": partial(smoothing_rows, "rows 2", 1),
                   "a transposed": quantised("a transposed", av, IC, sem("aq_up")),
                   "w2 transposed": quantised("w2 transposed", w2_in, IC, sem("dq_up")),
                   "w2 scale row": partial(scale_row, "w2 scale row", 1, 1),
                   "product 2": partial(product, "product 2", aqT, dqT, ("a transposed", "w2 transposed")),
                   "tokens A": partial(tokens, "tokens A", 0), "tokens B": partial(tokens, "tokens B", 1),
                   "scores A": partial(router, "scores A", 0, "tokens A"), "scores B": partial(router, "scores B", 1, "tokens B")})

        part1.close()

        K = TOPK

        def buf(name, shape, dt=F32):
            return ctx.enter_context(nc.sbuf_tensor(name, shape, dt))

        number = buf("number", [P, P, K * NT], F16)
        tile_number = buf("tile_number", [P, TILES])
        no_later = buf("no_later", [P, E, E])
        preference = buf("preference", [P, E])
        token = buf("token", [P, K, NT], F16)
        pad_row = buf("pad_row", [P, 1])
        prob = buf("prob", [P, NT, E])
        work = buf("work", [P, NT, E])
        best = buf("best", [P, K, NT])
        pick = buf("pick", [P, K, NT])
        chosen = buf("chosen", [P, K, NT, E])
        mask = buf("mask", [P, NT, E], BF16)
        total = buf("total", [P, NT])
        count = buf("count", [P, E])
        count_upto = buf("count_upto", [P, E, E])
        ends = buf("ends", [P, E])
        starts = buf("starts", [P, E])
        slot = buf("slot", [P, NT, E])
        pos = buf("pos", [P, K, NT])
        rounding = buf("rounding", [P, K, NT])
        slots = buf("slots", [P, K, NT * E])
        tile_of = buf("tile_of", [P, K, NT], F16)
        lane_of = buf("lane_of", [P, K, NT], F16)
        weight = buf("weight", [P, K, NT])
        weight_hi = buf("weight_hi", [P, K, NT], F16)
        weight_lo = buf("weight_lo", [P, K, NT], F16)
        in_lane = buf("in_lane", [P, P, K * NT], F16)
        in_tile = buf("in_tile", [P, TILES, K * NT], F16)
        packed = buf("packed", [P, 3, TILES, K * NT], F16)
        expert_of = buf("expert_of", [P, TILES])
        ended = buf("ended", [P, TILES, E])
        unused = buf("unused", [P, TILES])
        table = buf("table", [P, 3 * TILES])
        gather_idx = [buf(f"gather_idx{k}", [P, 1], I32) for k in range(2)]
        scatter_idx = [buf(f"scatter_idx{k}", [P, 1], I32) for k in range(2)]
        xg = [buf(f"xg{k}", [P, 2 * D], F16) for k in range(2)]
        xT = [buf(f"xT{k}", [P, 2, C, P], F16) for k in range(2)]
        gated = [buf(f"gated{k}", [P, F]) for k in range(2)]
        act_hl = [buf(f"act_hl{k}", [P, 2, F], F16) for k in range(2)]
        aT = [buf(f"aT{k}", [P, 2, FC, P], F16) for k in range(2)]
        y = [buf(f"y{k}", [P, D]) for k in range(2)]

        bank_x, bank_gu, bank_a, bank_y = bank_t, bank_r, bank_q, bank_h
        gu_hi_at, gu_lo_at = (t[:].rearrange("p e c f -> p (e c f)") for t in (gu_hi, gu_lo))
        dn_hi_at, dn_lo_at = (t[:].rearrange("p e c d -> p (e c d)") for t in (dn_hi, dn_lo))
        LAST = TILES - 1

        class Tile:

            def __init__(self, m, k):
                self.parity, self.half, self.i = k % 2, m + k // 2, 2 * m + k
                self.number = self.i if isinstance(self.i, int) else None

            def column(self, t):
                return t[:, self.i:self.i + 1] if self.number is not None else t[:, bass.ds(self.i, 1)]

        def over_tiles(eng, step):
            for k in range(3):
                step(0, k)
            with eng.Fori(1, (TILES - 3) // 2) as m:
                step(m, 1)
                step(m, 2)
            step(0, TILES - 2)
            step(0, TILES - 1)

        block = ctx.enter_context(nc.Block())

        @block.gpsimd
        def _(pool):
            def iota(t, pattern, base, step):
                pool.iota(t, pattern, base=base, channel_multiplier=step,
                          allow_small_or_imprecise_dtypes=True).then_inc(sem("numbers"), 1)

            iota(preference[:], [[-1, E]], E, 0)
            iota(token[:].rearrange("p k (b j) -> p k b j", b=B), [[0, K], [T, B], [1, J]], 1, J)
            iota(pad_row[:], [[0, 1]], N + 1, 1)
            iota(tile_number[:], [[1, TILES]], 0, 0)
            pool.memset(no_later[:], 1.0).then_inc(sem("ones_made"), 1)
            pool.wait_ge(sem("ones_made"), 1)
            pool.affine_select(out=no_later[:], in_=no_later[:], compare_op=ALU.is_ge, fill=0.0, base=0,
                               pattern=[[1, E], [-1, E]], channel_multiplier=0).then_inc(sem("numbers"), 1)
            iota(number[:], [[1, P], [0, K * NT]], 0, 0)

            def gather(m, k):
                t = Tile(m, k)
                if not (t.number is not None and t.number < 2):
                    pool.wait_ge(sem("x_filled"), t.i - 1)
                pool.tensor_copy(gather_idx[t.parity][:], t.column(gather_at)).then_inc(sem("gather_idx"), 1)
                pool.wait_ge(sem("gather_idx"), t.i + 1)
                hold(pool)
                pool.indirect_dma_start(out=xg[t.parity][:], out_offset=None, in_=halves_dram,
                                        in_offset=bass.IndirectOffsetOnAxis(ap=gather_idx[t.parity][:, 0:1], axis=0)
                                        ).then_inc(sem(f"gathered{t.parity}"), 16)

            def scatter(m, k):
                t = Tile(m, k)
                pool.tensor_copy(scatter_idx[t.parity][:], t.column(gather_at)).then_inc(sem("scatter_idx"), 1)
                pool.wait_ge(sem("scatter_idx"), t.i + 1)
                pool.wait_ge(sem("y_taken"), t.i + 1)
                if t.number != 0:
                    pool.wait_ge(sem("added"), 16 * t.i)
                hold(pool)
                pool.indirect_dma_start(out=out, out_offset=bass.IndirectOffsetOnAxis(ap=scatter_idx[t.parity][:, 0:1], axis=0),
                                        in_=y[t.parity][:], in_offset=None, compute_op=ALU.add).then_inc(sem("added"), 16)

            pool.wait_ge(sem("gather_ready"), 1)
            pool.wait_ge(sem("pad_stored"), 32)
            pool.wait_ge(sem("x1_stored"), 16 * B)
            pool.wait_ge(sem("halves_stored"), 16 * B)
            for k in range(3):
                gather(0, k)
            def step(m, k):
                t = Tile(m, k)
                if t.number is None or t.number + 3 < TILES:
                    gather(m, k + 3)
                if t.number != 0:
                    scatter(m, k - 1)
            for k in range(3):
                step(0, k)
            with pool.Fori(1, (TILES - 5) // 2) as m:
                step(m, 1)
                step(m, 2)
            for k in range(TILES - 4, TILES):
                step(0, k)
            scatter(0, LAST)
            pool.wait_ge(sem("added"), 16 * TILES)

        @block.vector
        def _(dve):
            steps = [0]

            def then(ins):
                steps[0] += 1
                ins.then_inc(sem("route"), 1)
                dve.wait_ge(sem("route"), steps[0])

            shape = [P, NT, E]
            dve.wait_ge(sem("numbers"), 5)
            then(dve.tensor_reduce(total[:], scores[:], AX.X, ALU.max))
            dve.tensor_tensor(work[:], scores[:], spread(total[:], shape, 2), ALU.subtract).then_inc(sem("shifted"), 1)
            dve.wait_ge(sem("exp_done"), 1)
            then(dve.tensor_reduce(total[:], prob[:], AX.X, ALU.add))
            then(dve.reciprocal(total[:], total[:]))
            then(dve.tensor_tensor(prob[:], prob[:], spread(total[:], shape, 2), ALU.mult))
            for k in range(K):
                then(dve.tensor_reduce(best[:, k], prob[:], AX.X, ALU.max))
                then(dve.tensor_tensor(work[:], prob[:], spread(best[:, k], shape, 2), ALU.is_equal))
                then(dve.tensor_tensor(work[:], work[:], spread(preference[:], shape, 1), ALU.mult))
                then(dve.tensor_reduce(pick[:, k], work[:], AX.X, ALU.max))
                then(dve.tensor_tensor(chosen[:, k], spread(preference[:], shape, 1), spread(pick[:, k], shape, 2), ALU.is_equal))
                if k == 0:
                    then(dve.scalar_tensor_tensor(out=prob[:], in0=chosen[:, 0], scalar=-2.0, in1=prob[:], op0=ALU.mult, op1=ALU.add))
            dve.tensor_tensor(mask[:], chosen[:, 0], chosen[:, 1], ALU.add).then_inc(sem("mask_ready"), 1)
            then(dve.tensor_tensor(total[:], best[:, 0], best[:, 1], ALU.add))
            then(dve.reciprocal(total[:], total[:]))
            then(dve.scalar_tensor_tensor(out=weight[:], in0=best[:], scalar=C_SCALE, in1=spread(total[:], [P, K, NT], 1),
                                          op0=ALU.mult, op1=ALU.mult))
            then(dve.tensor_copy(weight_hi[:], weight[:]))
            then(dve.tensor_tensor(weight_lo[:], weight[:], weight_hi[:], ALU.subtract))
            dve.wait_ge(sem("ranked"), 1)
            then(dve.tensor_scalar(count[:], bank_r[:, 0, NT * E:(NT + 1) * E], 1.0 / P, 0.5 - 0.5 / P, ALU.mult, ALU.add))
            then(dve.tensor_scalar(count[:], count[:], ROUND, ROUND, ALU.add, ALU.subtract))
            then(dve.tensor_tensor(count_upto[:], spread(count[:], [P, E, E], 1), no_later[:], ALU.mult))
            then(dve.tensor_reduce(ends[:], count_upto[:], AX.X, ALU.add))
            then(dve.tensor_tensor(starts[:], ends[:], count[:], ALU.subtract))
            then(dve.scalar_tensor_tensor(out=slot[:], in0=spread(starts[:], shape, 1), scalar=float(P),
                                          in1=bank_r[:, 0, 0:NT * E].rearrange("p (t e) -> p t e", e=E), op0=ALU.mult, op1=ALU.add))
            then(dve.tensor_tensor(slots[:], chosen[:].rearrange("p k t e -> p k (t e)"),
                                   spread(slot[:].rearrange("p t e -> p (t e)"), [P, K, NT * E], 1), ALU.mult))
            then(dve.tensor_reduce(pos[:], slots[:].rearrange("p k (t e) -> p k t e", e=E), AX.X, ALU.add))
            then(dve.tensor_scalar(rounding[:], pos[:], 1.0 / P, 0.5 / P - 0.5, ALU.mult, ALU.add))
            then(dve.tensor_scalar(tile_of[:], rounding[:], ROUND, ROUND, ALU.add, ALU.subtract))
            then(dve.scalar_tensor_tensor(out=lane_of[:], in0=tile_of[:], scalar=-float(P), in1=pos[:], op0=ALU.mult, op1=ALU.add))

            def per_tile(t, k):
                return spread(t[:, k], [P, TILES, NT], 1)

            dve.wait_ge(sem("numbers"), 6)
            for k in range(K):
                cols = slice(k * NT, (k + 1) * NT)
                dve.tensor_tensor(in_lane[:, :, cols], number[:, :, cols], spread(lane_of[:, k], [P, P, NT], 1), ALU.is_equal)
                then(dve.tensor_tensor(in_tile[:, :, cols], number[:, 0:TILES, cols], per_tile(tile_of, k), ALU.is_equal))
                dve.tensor_tensor(packed[:, 0, :, cols], in_tile[:, :, cols], per_tile(token, k), ALU.mult)
                dve.tensor_tensor(packed[:, 1, :, cols], in_tile[:, :, cols], per_tile(weight_hi, k), ALU.mult)
                dve.tensor_tensor(packed[:, 2, :, cols], in_tile[:, :, cols], per_tile(weight_lo, k), ALU.mult).then_inc(sem("packed"), 1)
            then(dve.tensor_tensor(ended[:], spread(ends[:], [P, TILES, E], 1), spread(tile_number[:], [P, TILES, E], 2), ALU.is_le))
            then(dve.tensor_reduce(expert_of[:], ended[:], AX.X, ALU.add))
            then(dve.tensor_scalar(expert_of[:], expert_of[:], float(E - 1), None, ALU.min))
            dve.tensor_scalar(gu_at[:], expert_of[:], float(C * 2 * F), None, ALU.mult).then_inc(sem("experts_known"), 1)
            dve.tensor_scalar(dn_at[:], expert_of[:], float(FC * D), None, ALU.mult).then_inc(sem("experts_known"), 1)
            dve.wait_ge(sem("sorted"), 1)
            then(dve.tensor_copy(table[:], bank_y[:, 0, 0:3 * TILES]))
            then(dve.tensor_scalar(unused[:], table[:, 0:TILES], 0.0, pad_row[:, 0:1], ALU.is_equal, ALU.mult))
            dve.scalar_tensor_tensor(out=gather_at[:], in0=table[:, 0:TILES], scalar=-1.0, in1=unused[:], op0=ALU.add,
                                     op1=ALU.add).then_inc(sem("gather_ready"), 1)
            then(dve.tensor_tensor(slot_weight[:], table[:, TILES:2 * TILES], table[:, 2 * TILES:], ALU.add))
            dve.tensor_scalar(slot_weight[:], slot_weight[:], 1.0 / (C_SCALE * A_SCALE), None, ALU.mult).then_inc(sem("weights_ready"), 1)

            def take_x(m, k):
                t = Tile(m, k)
                dve.wait_ge(sem("x_filled"), t.i + 1)
                if not (t.number is not None and t.number < 2):
                    dve.wait_ge(sem("gu_filled"), t.i - 1)
                dve.tensor_copy(xT[t.parity][:].rearrange("p h c t -> p (h c t)"),
                                bank_x[:, t.parity].bitcast(F16)).then_inc(sem("x_taken"), 1)

            def activate(m, k):
                t = Tile(m, k)
                dve.wait_ge(sem("gated"), t.i + 1)
                dve.scalar_tensor_tensor(out=gated[t.parity][:], in0=bank_gu[:, t.parity, F:2 * F], scalar=A_SCALE / X_SCALE,
                                         in1=gated[t.parity][:], op0=ALU.mult, op1=ALU.mult).then_inc(sem("gu_taken"), 1)
                dve.wait_ge(sem("act_hi"), t.i + 1)
                dve.tensor_tensor(act_hl[t.parity][:, 1], gated[t.parity][:], act_hl[t.parity][:, 0],
                                  ALU.subtract).then_inc(sem("act_lo"), 1)

            def step(m, k):
                t = Tile(m, k)
                if t.number is None or t.number < LAST:
                    take_x(m, k + 1)
                activate(m, k)

            take_x(0, 0)
            over_tiles(dve, step)

        @block.scalar
        def _(act):
            act.wait_ge(sem("shifted"), 1)
            act.activation(prob[:], work[:], ACT.Exp).then_inc(sem("exp_done"), 1)
            act.wait_ge(sem("exp_done"), 1)
            act.activation(gated[0][:, 0:1], identf[:, 0:1], ACT.Silu).then_inc(sem("warmed"), 1)
            act.wait_ge(sem("warmed"), 1)
            act.wait_ge(sem("weights_ready"), 1)

            def gate(m, k):
                t = Tile(m, k)
                act.wait_ge(sem("gu_filled"), t.i + 1)
                if not (t.number is not None and t.number < 2):
                    act.wait_ge(sem("act_lo"), t.i - 1)
                act.activation(gated[t.parity][:], bank_gu[:, t.parity, 0:F], ACT.Silu, scale=1.0 / X_SCALE).then_inc(sem("gated"), 1)
                act.wait_ge(sem("gu_taken"), t.i + 1)
                if not (t.number is not None and t.number < 2):
                    act.wait_ge(sem("a_filled"), t.i - 1)
                act.activation(act_hl[t.parity][:, 0], gated[t.parity][:], ACT.Copy).then_inc(sem("act_hi"), 1)

            def take_a(m, k):
                t = Tile(m, k)
                act.wait_ge(sem("a_filled"), t.i + 1)
                if not (t.number is not None and t.number < 2):
                    act.wait_ge(sem("y_filled"), t.i - 1)
                act.activation(aT[t.parity][:].rearrange("p h c t -> p (h c t)"),
                               bank_a[:, t.parity, 0:FC * P].bitcast(F16), ACT.Copy).then_inc(sem("a_taken"), 1)

            def take_y(m, k):
                t = Tile(m, k)
                act.wait_ge(sem("y_filled"), t.i + 1)
                if not (t.number is not None and t.number < 2):
                    act.wait_ge(sem("added"), 16 * (t.i - 1))
                act.activation(y[t.parity][:], bank_y[:, t.parity], ACT.Identity,
                               scale=t.column(slot_weight)).then_inc(sem("y_taken"), 1)

            def step(m, k):
                t = Tile(m, k)
                if t.number != 0:
                    take_a(m, k - 1)
                gate(m, k)
                if t.number != 0:
                    take_y(m, k - 1)

            over_tiles(act, step)
            take_a(0, LAST)
            take_y(0, LAST)

        @block.tensor
        def _(pe):
            pe.wait_ge(sem("mask_ready"), 1)
            rank = bank_r[:, 0, 0:(NT + 1) * E].rearrange("p (t e) -> p t e", e=E)
            pe.matmul(rank[:, 0:1], below[:], mask[:, 0:1], start=True, stop=True)
            for t in range(NT):
                ins = pe.matmul(rank[:, t + 1:], onesb[:], mask[:, t:t + 1].to_broadcast([P, NT - t, E]),
                                start=(t == 0), stop=(t == NT - 1))
                if t == 0:
                    pe.matmul(rank[:, 1:NT], below[:], mask[:, 1:], start=False, stop=False)
            ins.then_inc(sem("ranked"), 1)
            for n in range(K * NT):
                if n % NT == 0:
                    pe.wait_ge(sem("packed"), n // NT + 1)
                ins = pe.matmul(bank_y[:, 0, 0:3 * TILES], in_lane[:, :, n], packed[:, :, :, n],
                                start=(n == 0), stop=(n == K * NT - 1))
            ins.then_inc(sem("sorted"), 1)
            pe.wait_ge(sem("experts_known"), 2)
            pe.wait_ge(sem("weights_ready"), 1)

            def transpose_x(m, k):
                t = Tile(m, k)
                pe.wait_ge(sem(f"gathered{t.parity}"), 16 * (t.half + 1))
                if not (t.number is not None and t.number < 2):
                    pe.wait_ge(sem("x_taken"), t.i - 1)
                bank = bank_x[:, t.parity].bitcast(F16)
                for n in range(2 * C):
                    ins = pe.transpose(bank[:, n * P:(n + 1) * P], xg[t.parity][:, n * P:(n + 1) * P], identh[:])
                ins.then_inc(sem("x_filled"), 1)

            def gate_up(m, k, offset, chunks):
                t = Tile(m, k)
                if chunks[0] == 0:
                    pe.wait_ge(sem("x_taken"), t.i + 1)
                    if not (t.number is not None and t.number < 2):
                        pe.wait_ge(sem("gu_taken"), t.i - 1)
                for c in chunks:
                    cols = bass.ds(offset + c * 2 * F, 2 * F)
                    for n, (lhs, rhs) in enumerate(((0, gu_hi_at), (0, gu_lo_at), (1, gu_hi_at))):
                        ins = pe.matmul(bank_gu[:, t.parity], xT[t.parity][:, lhs, c], rhs[:, cols],
                                        start=(c == 0 and n == 0), stop=(c == C - 1 and n == 2))
                if chunks[-1] == C - 1:
                    ins.then_inc(sem("gu_filled"), 1)

            def transpose_a(m, k):
                t = Tile(m, k)
                pe.wait_ge(sem("act_lo"), t.i + 1)
                if not (t.number is not None and t.number < 2):
                    pe.wait_ge(sem("a_taken"), t.i - 1)
                bank = bank_a[:, t.parity].bitcast(F16)
                for n in range(2 * FC):
                    ins = pe.transpose(bank[:, n * P:(n + 1) * P], act_hl[t.parity][:, n // FC, n % FC * P:(n % FC + 1) * P], identh[:])
                ins.then_inc(sem("a_filled"), 1)

            def down(m, k, offset):
                t = Tile(m, k)
                pe.wait_ge(sem("a_taken"), t.i + 1)
                if not (t.number is not None and t.number < 2):
                    pe.wait_ge(sem("y_taken"), t.i - 1)
                for c in range(FC):
                    cols = bass.ds(offset + c * D, D)
                    for n, (lhs, rhs) in enumerate(((0, dn_hi_at), (0, dn_lo_at), (1, dn_hi_at))):
                        ins = pe.matmul(bank_y[:, t.parity], aT[t.parity][:, lhs, c], rhs[:, cols],
                                        start=(c == 0 and n == 0), stop=(c == FC - 1 and n == 2))
                ins.then_inc(sem("y_filled"), 1)

            def down_at(m, k):
                return pe.value_load(Tile(m, k).column(dn_at)[0:1], min_val=0, max_val=(E - 1) * FC * D)

            def step(m, k):
                t = Tile(m, k)
                if t.number is None or t.number < LAST:
                    transpose_x(m, k + 1)
                offset = pe.value_load(t.column(gu_at)[0:1], min_val=0, max_val=(E - 1) * C * 2 * F)
                gate_up(m, k, offset, range(0, C // 2))
                if t.number != 0:
                    down_offset = down_at(m, k - 1)
                    transpose_a(m, k - 1)
                gate_up(m, k, offset, range(C // 2, C))
                if t.number != 0:
                    down(m, k - 1, down_offset)

            transpose_x(0, 0)
            over_tiles(pe, step)
            transpose_a(0, LAST)
            down(0, LAST, down_at(0, LAST))


_INS = ["x", "fside_BxS2xS2_0", "ctx_1024", "L0_ffn_router_w", "L0_ffn_gate_proj", "L0_ffn_up_proj", "L0_ffn_down_proj"]


def kernel(**inputs):
    import numpy as np
    import concourse.bacc as bacc
    from concourse.bass_utils import run_bass_kernel_spmd

    nc = bacc.Bacc("TRN2", target_bir_lowering=False, num_devices=1)
    arrays, args = {}, []
    for name in _INS:
        a = np.ascontiguousarray(inputs[name])
        arrays[f"in_{name}"] = a
        args.append(nc.dram_tensor(f"in_{name}", a.shape, mybir.dt.from_np(a.dtype), kind="ExternalInput").ap())
    B, T, D = arrays["in_x"].shape
    args.append(nc.dram_tensor("out", (B * T + P, D), F32, kind="ExternalOutput").ap())
    block_kernel(nc, *args)
    result = run_bass_kernel_spmd(nc, [arrays], core_ids=[0]).results[0]["out"]
    return result[:B * T].reshape(B, T, D)
```
